# Optimizing a Trainium2 kernel written in Bass

```python
import numpy as np
import jax
import jax.numpy as jnp

def _softmax(x, axis=-1):
    return jax.nn.softmax(x, axis=axis)

def _gelu(x):
    return jax.nn.gelu(x, approximate=True)

def _silu(x):
    return jax.nn.silu(x)

def _sigmoid(x):
    return jax.nn.sigmoid(x)

def _layernorm(x, axis=-1, eps=1e-05):
    m = jnp.mean(x, axis=axis, keepdims=True)
    v = jnp.var(x, axis=axis, keepdims=True)
    return (x - m) / jnp.sqrt(v + eps)

def _scatter_add(tgt, idx, src, axis=0):
    return tgt.at[idx].add(src)

def _segment_sum(src, seg, n):
    return jax.ops.segment_sum(src, seg, n)
kernel_name = 'mk_audio_tower_d1_tok_audfeat1024_r4_01c68c'

def setup_inputs(seed: int=0):
    np.random.seed(seed)
    _w = jnp.asarray

    def _rec_inputs():
        import jax
        import jax.numpy as jnp
        _rk = jax.random.key(seed)
        x = -0.000125008 + 0.999885 * jax.random.normal(jax.random.fold_in(_rk, 1), (64, 256, 256), jnp.float32)
        return x
    x = _rec_inputs()

    def _L0_tok_setup():
        import jax, jax.numpy as jnp
        import numpy as np
        B, S, E, H = (4, 2048, 256, 16)
        D = E // H
        key = jax.random.key(seed)
        ks = jax.random.split(key, 9)
        s = 0.02
        return {'x': jax.random.normal(ks[0], (B, S, E), dtype=jnp.float32), 'Wq': jax.random.normal(ks[1], (D, E), dtype=jnp.float32) * s, 'bq': jax.random.normal(ks[2], (D,), dtype=jnp.float32) * s, 'Wk': jax.random.normal(ks[3], (D, E), dtype=jnp.float32) * s, 'bk': jax.random.normal(ks[4], (D,), dtype=jnp.float32) * s, 'Wv': jax.random.normal(ks[5], (D, E), dtype=jnp.float32) * s, 'bv': jax.random.normal(ks[6], (D,), dtype=jnp.float32) * s, 'Wo': jax.random.normal(ks[7], (E, E), dtype=jnp.float32) * s, 'bo': jax.random.normal(ks[8], (E,), dtype=jnp.float32) * s}
    _L0_tok_all = _L0_tok_setup()
    _L0_tok_in = {k: v for k, v in _L0_tok_all.items() if k in ('Wq', 'bq', 'Wk', 'bk', 'Wv', 'bv', 'Wo', 'bo')}
    del _L0_tok_all

    def _L0_attn_setup():
        import jax, jax.numpy as jnp
        import numpy as np
        import math
        B, N, D = (64, 128, 256)
        SHELL_DIM, RFF_DIM, ORDER = (64, 32, 4)
        CHARGE_COUPLING, SHELL_COUPLING = (1.0, 0.5)
        DIST_COUPLING, DIST_SCALE = (0.3, 10.0)
        COMBINED_DIM = 64

        def _forward(x, W_charge, b_charge, W_shell, b_shell, omega, rff_bias, W_combine, W_v, b_v, W_out, b_out, log_temp):
            b, n, d = x.shape
            q = jnp.tanh(x @ W_charge.T + b_charge)[..., 0]
            coeffs = jnp.asarray([(-CHARGE_COUPLING) ** m / math.factorial(m) for m in range(ORDER + 1)], dtype=x.dtype)
            mags = jnp.sqrt(jnp.abs(coeffs) + 1e-10)
            phi_c = mags * q[..., None] ** jnp.arange(ORDER + 1)
            shell = x @ W_shell.T + b_shell
            shell = shell / jnp.maximum(jnp.linalg.norm(shell, axis=-1, keepdims=True), 1e-12)
            proj = shell @ omega.T + rff_bias
            rff_scale = math.sqrt(2.0 / (2 * RFF_DIM)) * math.sqrt(math.exp(-SHELL_COUPLING))
            phi_s = jnp.concatenate([jnp.cos(proj), jnp.sin(proj)], axis=-1) * rff_scale
            tp = (phi_c[..., :, None] * phi_s[..., None, :]).reshape(b, n, -1)
            phi = tp @ W_combine.T
            idx = jnp.arange(n)
            T = jnp.exp(-DIST_COUPLING * jnp.abs(idx[:, None] - idx[None, :]).astype(x.dtype) / DIST_SCALE)
            temp = jax.nn.softplus(log_temp) + 0.1
            logits = jnp.einsum('bnd,bmd->bnm', phi, phi) * T / temp
            causal = idx[:, None] >= idx[None, :]
            logits = jnp.where(causal, logits, -jnp.inf)
            attn = jax.nn.softmax(logits, axis=-1)
            V = x @ W_v.T + b_v
            out = jnp.einsum('bnm,bmd->bnd', attn, V)
            return out @ W_out.T + b_out
        key = jax.random.key(seed)
        ks = jax.random.split(key, 12)
        s = 0.02
        inp = {'x': jax.random.normal(ks[0], (B, N, D), dtype=jnp.float32), 'W_charge': jax.random.normal(ks[1], (1, D), dtype=jnp.float32) * s, 'b_charge': jnp.zeros((1,), dtype=jnp.float32), 'W_shell': jax.random.normal(ks[2], (SHELL_DIM, D), dtype=jnp.float32) * s, 'b_shell': jnp.zeros((SHELL_DIM,), dtype=jnp.float32), 'omega': jax.random.normal(ks[3], (RFF_DIM, SHELL_DIM), dtype=jnp.float32) * math.sqrt(SHELL_COUPLING), 'rff_bias': jax.random.uniform(ks[4], (RFF_DIM,), dtype=jnp.float32) * (2.0 * math.pi), 'W_combine': jax.random.normal(ks[5], (COMBINED_DIM, (ORDER + 1) * 2 * RFF_DIM), dtype=jnp.float32) * s, 'W_v': jax.random.normal(ks[6], (D, D), dtype=jnp.float32) * s, 'b_v': jnp.zeros((D,), dtype=jnp.float32), 'W_out': jax.random.normal(ks[7], (D, D), dtype=jnp.float32) * s, 'b_out': jnp.zeros((D,), dtype=jnp.float32), 'log_temp': jnp.zeros((), dtype=jnp.float32)}
        return inp
    _L0_attn_all = _L0_attn_setup()
    _L0_attn_in = {k: v for k, v in _L0_attn_all.items() if k in ('W_charge', 'b_charge', 'W_shell', 'b_shell', 'omega', 'rff_bias', 'W_combine', 'W_v', 'b_v', 'W_out', 'b_out', 'log_temp')}
    del _L0_attn_all

    def _L0_ffn_setup():
        import jax, jax.numpy as jnp
        import numpy as np
        EPS = 1e-06
        LN_EPS = 1e-05

        def _absmean_core(W):
            gamma = jnp.mean(jnp.abs(W)) + EPS
            Ws = W / gamma
            Wq = jnp.sign(Ws) * jnp.minimum(jnp.round(jnp.abs(Ws)), 1.0)
            return (Wq, gamma)

        @jax.custom_vjp
        def absmean(W):
            return _absmean_core(W)[0]

        def _absmean_fwd(W):
            Wq, gamma = _absmean_core(W)
            return (Wq, gamma)

        def _absmean_bwd(gamma, g):
            return (g / gamma,)
        absmean.defvjp(_absmean_fwd, _absmean_bwd)

        def layernorm(x, w, b, eps=LN_EPS):
            mu = jnp.mean(x, axis=-1, keepdims=True)
            var = jnp.mean((x - mu) ** 2, axis=-1, keepdims=True)
            return (x - mu) * jax.lax.rsqrt(var + eps) * w + b
        key = jax.random.key(seed)
        k1, k2, k3 = jax.random.split(key, 3)
        d, h = (256, 1024)
        B, T = (8, 512)
        return {'x': jax.random.normal(k1, (B, T, d), jnp.float32), 'W_fc': jax.random.normal(k2, (h, d), jnp.float32), 'ln_w': jnp.ones((h,), jnp.float32), 'ln_b': jnp.zeros((h,), jnp.float32), 'W_proj': jax.random.normal(k3, (d, h), jnp.float32)}
    _L0_ffn_all = _L0_ffn_setup()
    _L0_ffn_in = {k: v for k, v in _L0_ffn_all.items() if k in ('W_fc', 'ln_w', 'ln_b', 'W_proj')}
    del _L0_ffn_all
    return {'x': x, 'L0_tok_Wq': _L0_tok_in['Wq'], 'L0_tok_bq': _L0_tok_in['bq'], 'L0_tok_Wk': _L0_tok_in['Wk'], 'L0_tok_bk': _L0_tok_in['bk'], 'L0_tok_Wv': _L0_tok_in['Wv'], 'L0_tok_bv': _L0_tok_in['bv'], 'L0_tok_Wo': _L0_tok_in['Wo'], 'L0_tok_bo': _L0_tok_in['bo'], 'L0_attn_W_charge': _L0_attn_in['W_charge'], 'L0_attn_b_charge': _L0_attn_in['b_charge'], 'L0_attn_W_shell': _L0_attn_in['W_shell'], 'L0_attn_b_shell': _L0_attn_in['b_shell'], 'L0_attn_omega': _L0_attn_in['omega'], 'L0_attn_rff_bias': _L0_attn_in['rff_bias'], 'L0_attn_W_combine': _L0_attn_in['W_combine'], 'L0_attn_W_v': _L0_attn_in['W_v'], 'L0_attn_b_v': _L0_attn_in['b_v'], 'L0_attn_W_out': _L0_attn_in['W_out'], 'L0_attn_b_out': _L0_attn_in['b_out'], 'L0_attn_log_temp': _L0_attn_in['log_temp'], 'L0_ffn_W_fc': _L0_ffn_in['W_fc'], 'L0_ffn_ln_w': _L0_ffn_in['ln_w'], 'L0_ffn_ln_b': _L0_ffn_in['ln_b'], 'L0_ffn_W_proj': _L0_ffn_in['W_proj']}

def reference(x, L0_tok_Wq, L0_tok_bq, L0_tok_Wk, L0_tok_bk, L0_tok_Wv, L0_tok_bv, L0_tok_Wo, L0_tok_bo, L0_attn_W_charge, L0_attn_b_charge, L0_attn_W_shell, L0_attn_b_shell, L0_attn_omega, L0_attn_rff_bias, L0_attn_W_combine, L0_attn_W_v, L0_attn_b_v, L0_attn_W_out, L0_attn_b_out, L0_attn_log_temp, L0_ffn_W_fc, L0_ffn_ln_w, L0_ffn_ln_b, L0_ffn_W_proj):
    import jax
    import jax.numpy as jnp

    def _L0_tok_ref(x, Wq, bq, Wk, bk, Wv, bv, Wo, bo):
        import jax, jax.numpy as jnp
        import numpy as np
        B, S, E, H = (4, 2048, 256, 16)
        D = E // H
        b, s, e = x.shape
        d = Wq.shape[0]
        h = e // d

        def split_heads(t):
            return t.reshape(b, -1, h, d).transpose(0, 2, 1, 3)
        q = split_heads(x @ Wq.T + bq)
        k = split_heads(x @ Wk.T + bk)
        v = split_heads(x @ Wv.T + bv)
        scores = jnp.einsum('bhqd,bhkd->bhqk', q, k) / np.sqrt(d).astype(jnp.float32)
        attn = jax.nn.softmax(scores, axis=-1)
        ctx = jnp.einsum('bhqk,bhkd->bhqd', attn, v)
        ctx = ctx.transpose(0, 2, 1, 3).reshape(b, -1, e)
        return ctx @ Wo.T + bo

    def _L0_attn_ref(x, W_charge, b_charge, W_shell, b_shell, omega, rff_bias, W_combine, W_v, b_v, W_out, b_out, log_temp):
        import jax, jax.numpy as jnp
        import numpy as np
        import math
        B, N, D = (64, 128, 256)
        SHELL_DIM, RFF_DIM, ORDER = (64, 32, 4)
        CHARGE_COUPLING, SHELL_COUPLING = (1.0, 0.5)
        DIST_COUPLING, DIST_SCALE = (0.3, 10.0)
        COMBINED_DIM = 64

        def _forward(x, W_charge, b_charge, W_shell, b_shell, omega, rff_bias, W_combine, W_v, b_v, W_out, b_out, log_temp):
            b, n, d = x.shape
            q = jnp.tanh(x @ W_charge.T + b_charge)[..., 0]
            coeffs = jnp.asarray([(-CHARGE_COUPLING) ** m / math.factorial(m) for m in range(ORDER + 1)], dtype=x.dtype)
            mags = jnp.sqrt(jnp.abs(coeffs) + 1e-10)
            phi_c = mags * q[..., None] ** jnp.arange(ORDER + 1)
            shell = x @ W_shell.T + b_shell
            shell = shell / jnp.maximum(jnp.linalg.norm(shell, axis=-1, keepdims=True), 1e-12)
            proj = shell @ omega.T + rff_bias
            rff_scale = math.sqrt(2.0 / (2 * RFF_DIM)) * math.sqrt(math.exp(-SHELL_COUPLING))
            phi_s = jnp.concatenate([jnp.cos(proj), jnp.sin(proj)], axis=-1) * rff_scale
            tp = (phi_c[..., :, None] * phi_s[..., None, :]).reshape(b, n, -1)
            phi = tp @ W_combine.T
            idx = jnp.arange(n)
            T = jnp.exp(-DIST_COUPLING * jnp.abs(idx[:, None] - idx[None, :]).astype(x.dtype) / DIST_SCALE)
            temp = jax.nn.softplus(log_temp) + 0.1
            logits = jnp.einsum('bnd,bmd->bnm', phi, phi) * T / temp
            causal = idx[:, None] >= idx[None, :]
            logits = jnp.where(causal, logits, -jnp.inf)
            attn = jax.nn.softmax(logits, axis=-1)
            V = x @ W_v.T + b_v
            out = jnp.einsum('bnm,bmd->bnd', attn, V)
            return out @ W_out.T + b_out
        return _forward(x, W_charge, b_charge, W_shell, b_shell, omega, rff_bias, W_combine, W_v, b_v, W_out, b_out, log_temp)

    def _L0_ffn_ref(x, W_fc, ln_w, ln_b, W_proj):
        import jax, jax.numpy as jnp
        import numpy as np
        EPS = 1e-06
        LN_EPS = 1e-05

        def _absmean_core(W):
            gamma = jnp.mean(jnp.abs(W)) + EPS
            Ws = W / gamma
            Wq = jnp.sign(Ws) * jnp.minimum(jnp.round(jnp.abs(Ws)), 1.0)
            return (Wq, gamma)

        @jax.custom_vjp
        def absmean(W):
            return _absmean_core(W)[0]

        def _absmean_fwd(W):
            Wq, gamma = _absmean_core(W)
            return (Wq, gamma)

        def _absmean_bwd(gamma, g):
            return (g / gamma,)
        absmean.defvjp(_absmean_fwd, _absmean_bwd)

        def layernorm(x, w, b, eps=LN_EPS):
            mu = jnp.mean(x, axis=-1, keepdims=True)
            var = jnp.mean((x - mu) ** 2, axis=-1, keepdims=True)
            return (x - mu) * jax.lax.rsqrt(var + eps) * w + b
        h = jnp.einsum('btd,hd->bth', x, absmean(W_fc))
        h = jax.nn.gelu(h, approximate=False)
        h = layernorm(h, ln_w, ln_b)
        return jnp.einsum('bth,dh->btd', h, absmean(W_proj))
    h = _L0_tok_ref(x, L0_tok_Wq, L0_tok_bq, L0_tok_Wk, L0_tok_bk, L0_tok_Wv, L0_tok_bv, L0_tok_Wo, L0_tok_bo)
    h = h + _L0_attn_ref(_layernorm(h, axis=-1), L0_attn_W_charge, L0_attn_b_charge, L0_attn_W_shell, L0_attn_b_shell, L0_attn_omega, L0_attn_rff_bias, L0_attn_W_combine, L0_attn_W_v, L0_attn_b_v, L0_attn_W_out, L0_attn_b_out, L0_attn_log_temp)
    h = h + _L0_ffn_ref(_layernorm(h, axis=-1), L0_ffn_W_fc, L0_ffn_ln_w, L0_ffn_ln_b, L0_ffn_W_proj)
    return h

_drawn_inputs = setup_inputs


def setup_inputs(seed=0):
    import zlib

    import numpy as np

    out = dict(_drawn_inputs(seed))
    spreads = {'L0_attn_b_shell': (0.0, 2.0),
     'L0_attn_b_v': (0.0, 0.1),
     'L0_attn_b_out': (0.0, 0.1),
     'L0_ffn_ln_w': (1.0, 0.2),
     'L0_ffn_ln_b': (0.0, 0.1)}
    factors = {'L0_tok_bq': 8.0,
     'L0_tok_bk': 64.0,
     'L0_attn_W_charge': 64.0,
     'L0_attn_W_shell': 64.0,
     'L0_attn_omega': 64.0,
     'L0_attn_rff_bias': 64.0,
     'L0_attn_W_combine': 64.0}
    for name, (base, spread) in spreads.items():
        noise = np.random.default_rng([zlib.crc32(name.encode()), seed]).standard_normal(out[name].shape)
        drawn = base * np.exp(spread * noise) if base else spread * noise
        out[name] = jnp.asarray(drawn.astype(out[name].dtype))
    for name, factor in factors.items():
        out[name] = (out[name] * factor).astype(out[name].dtype)
    return out
```

```python
from collections import namedtuple
from contextlib import ExitStack
import math

import concourse.bass as bass
from concourse import mybir

F32 = mybir.dt.float32
FR = mybir.dt.float32r
ALU = mybir.AluOpType
ACT = mybir.ActivationFunctionType
AX = mybir.AxisListType

P = 128
E = 256
KT = E // P
B, S = 64, 256
H, D = 16, 16
N = S // H
HQ, HM, HL = 4, 2, 2
HP = P // 2
HH = HP // N
TILES = 8
LAGS = 3
TB = B // TILES
G = TB * HM
C = G * N
SH = 64
RF = 64
CD = 64
ORDER = 4
HID = 1024
HC = HID // P
PW = E + SH + 1
EPS = 1e-5
TINY = 1e-24
MAGIC = 1.5 * 2.0 ** 23
TWO_PI_HI = 6.28125
TWO_PI_LO = 2.0 * math.pi - TWO_PI_HI
HALF_PI = 0.5 * math.pi
PI_IN = 3.141592
RFF_SCALE = math.sqrt(2.0 / RF) * math.sqrt(math.exp(-0.5))
MAGS = [math.sqrt(1.0 / math.factorial(m) + 1e-10) for m in range(ORDER + 1)]

COL_MASK = 0
COL_BQ, COL_BK, COL_BV = HH, HH + 1, HH + 2
COL_RB = HH + 3
COL_OFF = HH + 4
COL_SHIFT = HH + 5
COL_HI, COL_LO = HH + 6, HH + 7
COL_MBV = HH + 8
COL_LNB = COL_MBV + KT
COLS = COL_LNB + HC

PACK = {}
PACKED = 0
for _name, _width in (("ident", P), ("w_o", HL * E), ("b_o", E), ("m_out", KT * E), ("m_v", KT * E),
                      ("m_shell", KT * (SH + 1)), ("b_out", E), ("b_shell", SH + 1), ("temp", 1),
                      ("decay", P), ("hidden", P)):
    PACK[_name] = (PACKED, PACKED + _width)
    PACKED += _width

Tile = namedtuple("Tile", "t par pair")


def first(o):
    return isinstance(o.t, int) and o.t == 0


def after(eng, sem, count):
    if not (isinstance(count, int) and count <= 0):
        eng.wait_ge(sem, count)


def settle(eng):
    eng.nop(nofuse=True)


def steps(eng, step, loop_from=4):
    def run(i, n):
        def do(operation, lag, *which):
            k = n - lag
            if isinstance(i, int):
                if 0 <= k < TILES:
                    operation(Tile(k, k % 2, k // 2), *which)
            else:
                operation(Tile(2 * i + k, k % 2, i + k // 2), *which)

        def once(setup, at):
            if isinstance(i, int) and n == at:
                setup()
        step(do, once)

    for s in range(loop_from):
        run(0, s)
    with eng.Fori(0, 2) as i:
        run(i, loop_from)
        run(i, loop_from + 1)
    for s in range(loop_from + 4, TILES + LAGS):
        run(0, s)


def audio_tower(nc, x, cols, w_qkv, packed, omega, w_comb, w_fc, w_proj, ln_w, out):
    with ExitStack() as ctx:
        def sb(name, shape, dt=F32):
            return ctx.enter_context(nc.sbuf_tensor(name, shape, dt))

        def sem(name):
            return ctx.enter_context(nc.semaphore(name))

        col = sb("col", [P, COLS])
        wq = sb("wq", [P, 2, KT, HL, 2 * D])
        bqm = sb("bqm", [P, HH])
        pk = sb("pk", [P, PACKED])
        bvw = sb("bvw", [P, KT, P])
        w2 = sb("w2", [P, KT, PW])
        b2 = sb("b2", [P, PW])
        om = sb("om", [SH, RF])
        wc_raw = sb("wc_raw", [RF, ORDER + 1, CD])
        wc = sb("wc", [RF, ORDER + 1, CD])
        fc_raw = sb("fc_raw", [P, KT, HID])
        pr_raw = sb("pr_raw", [P, HC, E])
        below = sb("below", [P, 2048])
        fc = sb("fc", [P, KT, HID], FR)
        pr = sb("pr", [P, HC, E], FR)
        absum = sb("absum", [P, 2])
        thr = sb("thr", [P, 4])
        lnw = sb("lnw", [P, HID])
        lnbw = sb("lnbw", [P, HC, P])
        b3 = sb("b3", [P, E])
        ones = sb("ones", [P, P])
        dec = sb("dec", [P, P])
        tmp = sb("tmp", [P, 8])
        mhalf = sb("mhalf", [P, 1])

        def part(name):
            return pk[:, PACK[name][0]:PACK[name][1]]

        idn, bo, hid = part("ident"), part("b_o"), part("hidden")
        wo = part("w_o").rearrange("p (l e) -> p l e", l=HL)
        mo = part("m_out").rearrange("p (k e) -> p k e", k=KT)
        mv = part("m_v").rearrange("p (k e) -> p k e", k=KT)

        xt = [sb(f"xt{i}", [P, HL, KT, HQ, C]) for i in range(2)]
        qm = sb("qm", [P, G, HH, N])
        ks = sb("ks", [P, G, N])
        qt = sb("qt", [P, TB, HL, 2 * D])
        vm = sb("vm", [P, G, HH, D])
        smax = sb("smax", [P, G])
        sc = sb("sc", [P, G, N])
        pe_ = sb("pe_", [P, G, N])
        ssum = sb("ssum", [P, G])
        srec = sb("srec", [P, G])
        pn = sb("pn", [P, G, N])
        pt = sb("pt", [P, G, N])
        cx = sb("cx", [P, HL, TB, N])
        h0 = [sb(f"h0_{i}", [P, E]) for i in range(2)]
        st1 = sb("st1", [P, 6])
        mv1 = sb("mv1", [P, 2])
        rs1 = sb("rs1", [P, 2])
        z1 = sb("z1", [P, E])
        z1t = sb("z1t", [P, KT, P])
        pj = [sb(f"pj{i}", [P, PW]) for i in range(2)]
        qc = [sb(f"qc{i}", [P, 1]) for i in range(2)]
        sq = sb("sq", [P, SH])
        nn = sb("nn", [P, 3])
        un = sb("un", [P, SH])
        unt = sb("unt", [SH, P])
        ang = sb("ang", [RF, 5, P])
        ft = sb("ft", [RF, P])
        yy = sb("yy", [P, ORDER + 1, CD])
        ho = sb("ho", [P, ORDER, CD])
        pht = sb("pht", [CD, P])
        lg = sb("lg", [P, 2, P])
        nmx = sb("nmx", [P, 1])
        at = sb("at", [P, P])
        asum = sb("asum", [P, 2])
        att = sb("att", [P, P])
        h1 = [sb(f"h1_{i}", [P, E]) for i in range(2)]
        st2 = sb("st2", [P, 6])
        mv2 = sb("mv2", [P, 2])
        rs2 = [sb(f"rs2_{i}", [P, 2]) for i in range(2)]
        z2 = sb("z2", [P, E])
        z2h = sb("z2h", [P, KT, P], FR)
        z2l = sb("z2l", [P, KT, P], FR)
        gl = sb("gl", [P, HID])
        st3 = sb("st3", [P, 12])
        mv3 = sb("mv3", [P, 2])
        rs3 = sb("rs3", [P, 2])
        gn = sb("gn", [P, HID])
        gh = sb("gh", [P, HC, P], FR)
        glo = sb("glo", [P, HC, P], FR)
        res = sb("res", [P, E])

        def bank(name):
            return ctx.enter_context(nc.psum_tensor(name, [P, 512], F32))

        p_qv, p_k, p_a0, p_a1, p_m0, p_m1 = [bank(n) for n in ("p_qv", "p_k", "p_a0", "p_a1", "p_m0", "p_m1")]
        p_f = ctx.enter_context(nc.psum_tensor("p_f", [P, 2, 512], F32))

        x_in = [[sem(f"x_in{i}{j}") for j in range(HL)] for i in range(2)]
        in_qkv, in_pack, in_feat, in_ffn = sem("in_qkv"), sem("in_pack"), sem("in_feat"), sem("in_ffn")
        bqm_ready, half_set, ones_set = sem("bqm_ready"), sem("half_set"), sem("ones_set")
        temp_act, temp_dve, dec_ready, wc_ready = sem("temp_act"), sem("temp_dve"), sem("dec_ready"), sem("wc_ready")
        bvw_ready, w2_made, w2_ready = sem("bvw_ready"), sem("w2_made"), sem("w2_ready")
        abs_summed, abs_total, thr_steps = sem("abs_summed"), sem("abs_total"), sem("thr_steps")
        below_ready, ffn_ready = sem("below_ready"), sem("ffn_ready")
        lnbw_ready, b3_made, b3_ready = sem("lnbw_ready"), sem("b3_made"), sem("b3_ready")
        qv_ready, k_ready, q_kept, k_kept = sem("qv_ready"), sem("k_ready"), sem("q_kept"), sem("k_kept")
        v_turned, v_masked = sem("v_turned"), sem("v_masked")
        s_ready, s_max, s_less, s_exp = sem("s_ready"), sem("s_max"), sem("s_less"), sem("s_exp")
        s_sum, s_rec, p_ready, p_turned = sem("s_sum"), sem("s_rec"), sem("p_ready"), sem("p_turned")
        c_ready, c_kept, h0_ready, h0_kept = sem("c_ready"), sem("c_kept"), sem("h0_ready"), sem("h0_kept")
        st1_ready, mv1_ready, var1_ready, rs1_ready = sem("st1_ready"), sem("mv1_ready"), sem("var1_ready"), sem("rs1_ready")
        z1_ready, z1t_ready, z1t_kept = sem("z1_ready"), sem("z1t_ready"), sem("z1t_kept")
        pj_ready, pj_kept, charge_ready = sem("pj_ready"), sem("pj_kept"), sem("charge_ready")
        n2_ready, floor_ready, rn_ready, un_ready = sem("n2_ready"), sem("floor_ready"), sem("rn_ready"), sem("un_ready")
        unt_ready, unt_kept, an_ready, an_steps = sem("unt_ready"), sem("unt_kept"), sem("an_ready"), sem("an_steps")
        ft_ready = sem("ft_ready")
        y_ready, y_kept, phi_steps = sem("y_ready"), sem("y_kept"), sem("phi_steps")
        pht_ready, pht_kept, gram_ready = sem("pht_ready"), sem("pht_kept"), sem("gram_ready")
        lg_ready, lg_max, at_ready, arec_ready = sem("lg_ready"), sem("lg_max"), sem("at_ready"), sem("arec_ready")
        att_ready, att_kept, mixed_ready, h1_ready = sem("att_ready"), sem("att_kept"), sem("mixed_ready"), sem("h1_ready")
        st2_ready, mv2_ready, var2_ready, rs2_ready = sem("st2_ready"), sem("mv2_ready"), sem("var2_ready"), sem("rs2_ready")
        z2_ready, z2t_ready, z2h_ready, z2l_ready = sem("z2_ready"), sem("z2t_ready"), sem("z2h_ready"), sem("z2l_ready")
        fc_ready, gl_ready, st3_ready, mv3_ready = sem("fc_ready"), sem("gl_ready"), sem("st3_ready"), sem("mv3_ready")
        var3_ready, rs3_ready, gn_ready, gt_ready = sem("var3_ready"), sem("rs3_ready"), sem("gn_ready"), sem("gt_ready")
        gh_ready, glo_ready, h1_biased = sem("gh_ready"), sem("glo_ready"), sem("h1_biased")
        ff_ready, res_ready, stored = sem("ff_ready"), sem("res_ready"), sem("stored")

        block = ctx.enter_context(nc.Block())

        @block.sync
        def _(sp):
            def load(o):
                for j in range(HL):
                    after(sp, qv_ready, o.t - 1)
                    after(sp, k_ready, o.t - 1)
                    sp.dma_start(xt[o.par][:, j], x[o.t, :, j]).then_inc(x_in[o.par][j], 16)

            def load_pack():
                sp.dma_start(pk[:, :], packed).then_inc(in_pack, 16)

            def load_rest():
                sp.dma_start(om[:, :], omega).then_inc(in_feat, 16)
                sp.dma_start(wc_raw[:, :, :], w_comb).then_inc(in_feat, 16)
                sp.dma_start(fc_raw[:, :, :], w_fc).then_inc(in_ffn, 16)
                sp.dma_start(pr_raw[:, :, :], w_proj).then_inc(in_ffn, 16)
                sp.dma_start(lnw[:, :], ln_w).then_inc(in_ffn, 16)

            def store(o):
                sp.wait_ge(res_ready, o.t + 1)
                sp.dma_start(out[o.t], res[:, :]).then_inc(stored, 16)

            def step(do, once):
                once(load_pack, 0)
                do(load, -1)
                once(load_rest, 0)
                do(store, 3)

            sp.dma_start(wq[:, :, :, :, :], w_qkv).then_inc(in_qkv, 16)
            sp.dma_start(col[:, :], cols).then_inc(in_qkv, 16)
            load(Tile(0, 0, 0))
            steps(sp, step, loop_from=3)
            sp.wait_ge(stored, 16 * TILES)

        @block.gpsimd
        def _(pool):
            pool.memset(mhalf[:, :], -0.5).then_inc(half_set, 1)
            pool.memset(ones[:, :], 1.0).then_inc(ones_set, 1)
            pool.wait_ge(half_set, 1)

            def repeat_biases():
                pool.wait_ge(ones_set, 1)
                pool.wait_ge(in_qkv, 32)
                for k in range(KT):
                    last = pool.tensor_scalar(bvw[:, k, :], ones[:, :], col[:, COL_MBV + k:COL_MBV + k + 1], None, ALU.mult)
                last.then_inc(bvw_ready, 1)
                for m in range(HC):
                    last = pool.tensor_scalar(lnbw[:, m, :], ones[:, :], col[:, COL_LNB + m:COL_LNB + m + 1], None, ALU.mult)
                last.then_inc(lnbw_ready, 1)

            def root1(o):
                pool.wait_ge(mv1_ready, o.t + 1)
                after(pool, pj_kept, o.t)
                settle(pool)
                pool.tensor_scalar(rs1[:, 0:1], mv1[:, 1:2], EPS, None, ALU.add).then_inc(var1_ready, 1)
                pool.wait_ge(var1_ready, o.t + 1)
                pool.tensor_tensor(rs1[:, 1:2], rs1[:, 0:1], mhalf[:, :], ALU.pow).then_inc(rs1_ready, 1)

            def root2(o):
                pool.wait_ge(mv2_ready, o.t + 1)
                after(pool, gl_ready, 2 * (o.t - 1))
                settle(pool)
                rs = rs2[o.par]
                pool.tensor_scalar(rs[:, 0:1], mv2[:, 1:2], EPS, None, ALU.add).then_inc(var2_ready, 1)
                pool.wait_ge(var2_ready, o.t + 1)
                pool.tensor_tensor(rs[:, 1:2], rs[:, 0:1], mhalf[:, :], ALU.pow).then_inc(rs2_ready, 1)

            def bias_residual(o):
                if first(o):
                    pool.wait_ge(b3_ready, 1)
                pool.wait_ge(z2_ready, o.t + 1)
                pool.tensor_tensor(h1[o.par][:, :], h1[o.par][:, :], b3[:, :], ALU.add).then_inc(h1_biased, 1)

            def root_norm(o):
                pool.wait_ge(n2_ready, o.t + 1)
                after(pool, un_ready, o.t)
                settle(pool)
                pool.tensor_scalar(nn[:, 1:2], nn[:, 0:1], TINY, None, ALU.max).then_inc(floor_ready, 1)
                pool.wait_ge(floor_ready, o.t + 1)
                pool.tensor_tensor(nn[:, 2:3], nn[:, 1:2], mhalf[:, :], ALU.pow).then_inc(rn_ready, 1)

            def root3(o):
                pool.wait_ge(mv3_ready, o.t + 1)
                after(pool, res_ready, o.t)
                settle(pool)
                pool.tensor_scalar(rs3[:, 0:1], mv3[:, 1:2], EPS, None, ALU.add).then_inc(var3_ready, 1)
                pool.wait_ge(var3_ready, o.t + 1)
                pool.tensor_tensor(rs3[:, 1:2], rs3[:, 0:1], mhalf[:, :], ALU.pow).then_inc(rs3_ready, 1)

            def step(do, once):
                do(root_norm, 2)
                do(root2, 3)
                once(repeat_biases, 0)
                do(bias_residual, 3)
                do(root1, 1)
                do(root3, 3)

            steps(pool, step)

        @block.scalar
        def _(act):
            a = nc.scalar.activation

            def temperature():
                act.wait_ge(in_pack, 16)
                a(tmp[:, 1:2], part("temp"), ACT.Abs).then_inc(temp_act, 1)
                act.wait_ge(temp_act, 1)
                a(tmp[:, 2:3], tmp[:, 1:2], ACT.Exp, scale=-1.0).then_inc(temp_act, 1)
                act.wait_ge(temp_act, 2)
                a(tmp[:, 3:4], tmp[:, 2:3], ACT.Ln, bias=1.0).then_inc(temp_act, 1)

            def magnitudes():
                act.wait_ge(in_ffn, 48)
                a(below[:, :], fc_raw[:, :, :], ACT.Abs, accum_out=absum[:, 0:1]).then_inc(abs_summed, 1)
                act.wait_ge(abs_summed, 1)
                a(below[:, :], pr_raw[:, :, :], ACT.Abs, accum_out=absum[:, 1:2]).then_inc(abs_summed, 1)

            def keep_q(o):
                act.wait_ge(v_turned, o.t + 1)
                after(act, s_ready, o.t)
                if first(o):
                    act.wait_ge(bqm_ready, 1)
                for h in range(HH):
                    l = h % HL
                    last = a(qm[:, :, h, :], p_qv[:, C * l:C * l + C].rearrange("p (g n) -> p g n", g=G), ACT.Identity,
                             bias=bqm[:, h:h + 1], scale=col[:, COL_MASK + h:COL_MASK + h + 1])
                last.then_inc(q_kept, 1)

            def keep_k(o):
                act.wait_ge(k_ready, o.t + 1)
                after(act, s_ready, o.t)
                a(ks[:, :, :], p_k[:, 0:C].rearrange("p (g n) -> p g n", g=G), ACT.Identity,
                  bias=col[:, COL_BK:COL_BK + 1]).then_inc(k_kept, 1)

            def exp_scores(o):
                act.wait_ge(s_less, o.t + 1)
                after(act, p_ready, o.t)
                a(pe_[:, :, :], sc[:, :, :], ACT.Exp, scale=D ** -0.5).then_inc(s_exp, 1)

            def keep_context(o):
                act.wait_ge(c_ready, o.t + 1)
                after(act, h0_ready, o.t)
                a(cx[:, :, :, :], p_a1[:, 0:C].rearrange("p (b l i) -> p l b i", b=TB, l=HL), ACT.Identity,
                  bias=col[:, COL_BV:COL_BV + 1]).then_inc(c_kept, 1)

            def keep_z1(o):
                act.wait_ge(z1t_ready, o.t + 1)
                after(act, pj_ready, o.t)
                a(z1t[:, :, :], p_a1[:, 0:E].rearrange("p (k n) -> p k n", k=KT), ACT.Copy).then_inc(z1t_kept, 1)

            def charge(o):
                act.wait_ge(pj_kept, o.t + 1)
                after(act, phi_steps, ORDER * (o.t - 1))
                a(qc[o.par][:, :], pj[o.par][:, PW - 1:PW], ACT.Tanh).then_inc(charge_ready, 1)

            def keep_unit(o):
                act.wait_ge(unt_ready, o.t + 1)
                after(act, an_ready, o.t)
                a(unt[:, :], p_a1[0:SH, 0:P], ACT.Copy).then_inc(unt_kept, 1)

            def sines(o):
                act.wait_ge(an_steps, 6 * o.t + 6)
                after(act, y_ready, o.t)
                a(ft[:, :], ang[:, 4, :], ACT.Sin, bias=col[0:RF, COL_SHIFT:COL_SHIFT + 1]).then_inc(ft_ready, 1)

            def keep_powers(o):
                act.wait_ge(y_ready, o.t + 1)
                after(act, phi_steps, ORDER * o.t)
                a(yy[:, :, :], p_m1[:, 0:(ORDER + 1) * CD], ACT.Copy).then_inc(y_kept, 1)

            def keep_phi(o):
                act.wait_ge(pht_ready, o.t + 1)
                after(act, gram_ready, o.t)
                a(pht[:, :], p_m0[0:CD, 0:P], ACT.Copy).then_inc(pht_kept, 1)

            def exp_logits(o):
                act.wait_ge(lg_max, o.t + 1)
                after(act, att_ready, o.t)
                after(act, arec_ready, o.t)
                a(at[:, :], lg[:, 1, :], ACT.Exp, bias=nmx[:, :], scale=-1.0, accum_out=asum[:, 0:1]).then_inc(at_ready, 1)

            def keep_weights(o):
                act.wait_ge(att_ready, o.t + 1)
                after(act, mixed_ready, o.t)
                a(att[:, :], p_m0[:, 0:P], ACT.Copy).then_inc(att_kept, 1)

            def gelu(o, j):
                act.wait_ge(fc_ready, 2 * o.t + j + 1)
                if j == 0:
                    after(act, gn_ready, o.t)
                    act.wait_ge(rs2_ready, o.t + 1)
                a(gl[:, 512 * j:512 * j + 512], p_f[:, j, :], ACT.Gelu, scale=rs2[o.par][:, 1:2]).then_inc(gl_ready, 1)

            def high_z2(o):
                act.wait_ge(z2t_ready, o.t + 1)
                after(act, fc_ready, 2 * o.t)
                a(z2h[:, :, :], p_m0[:, 0:E].rearrange("p (k n) -> p k n", k=KT), ACT.Copy).then_inc(z2h_ready, 1)

            def high_hidden(o, j):
                act.wait_ge(gt_ready, 2 * o.t + j + 1)
                after(act, ff_ready, o.t)
                a(gh[:, 4 * j:4 * j + 4, :], p_f[:, j, :].rearrange("p (m n) -> p m n", n=P), ACT.Copy).then_inc(gh_ready, 1)

            def step(do, once):
                do(keep_context, 1)
                do(high_z2, 3)
                do(keep_powers, 2)
                do(gelu, 3, 0)
                once(magnitudes, 1)
                do(keep_z1, 1)
                do(gelu, 3, 1)
                do(keep_phi, 2)
                do(keep_q, 0)
                do(keep_k, 0)
                do(charge, 1)
                do(keep_unit, 1)
                do(exp_logits, 2)
                do(high_hidden, 3, 0)
                once(temperature, 0)
                do(exp_scores, 0)
                do(keep_weights, 2)
                do(high_hidden, 3, 1)
                do(sines, 1)

            act.wait_ge(in_qkv, 32)
            steps(act, step)

        @block.tensor
        def _(pe):
            mm = nc.tensor.matmul

            def stacked(o, which, bank_, base, l, start, stop):
                for k in range(KT):
                    for q in range(HQ):
                        last = mm(bank_[32 * q:32 * q + 32, base:base + C], wq[:, which, k, l, :], xt[o.par][:, l, k, q, :],
                                  start=(start and k == 0), stop=(stop and k == KT - 1))
                return last

            def project_qv(o, l):
                pe.wait_ge(x_in[o.par][l], 16 * (o.pair + 1))
                if l == 0:
                    after(pe, q_kept, o.t)
                last = stacked(o, 0, p_qv, C * l, l, True, True)
                if l == HL - 1:
                    last.then_inc(qv_ready, 1)

            def project_k(o, l):
                pe.wait_ge(x_in[o.par][l], 16 * (o.pair + 1))
                if l == 0:
                    after(pe, k_kept, o.t)
                last = stacked(o, 1, p_k, 0, l, l == 0, l == HL - 1)
                if l == HL - 1:
                    last.then_inc(k_ready, 1)

            def blocks(bank_, stationary, moving, signal):
                for g in range(G):
                    for h in range(0, P, HP):
                        last = mm(bank_[h:h + HP, N * g:N * g + N],
                                  stationary[h:h + HP, g, :, :].rearrange("p a d -> p (a d)"),
                                  moving[h:h + HP, g, :], start=True, stop=True)
                last.then_inc(signal, 1)

            def scores(o):
                pe.wait_ge(q_kept, o.t + 1)
                pe.wait_ge(k_kept, o.t + 1)
                after(pe, pj_kept, o.t)
                settle(pe)
                blocks(p_a0, qm, ks, s_ready)

            def context(o):
                pe.wait_ge(p_turned, o.t + 1)
                pe.wait_ge(v_masked, o.t + 1)
                after(pe, an_steps, 6 * o.t)
                settle(pe)
                blocks(p_a1, vm, pt, c_ready)

            def join_heads(o):
                if first(o):
                    pe.wait_ge(in_pack, 16)
                pe.wait_ge(c_kept, o.t + 1)
                pe.wait_ge(s_less, o.t + 1)
                for l in range(HL):
                    last = mm(p_a0[:, 0:E], cx[:, l, :, :].rearrange("p b i -> p (b i)"), wo[:, l, :],
                              start=(l == 0), stop=(l == HL - 1))
                last.then_inc(h0_ready, 1)

            def turn_z1(o):
                pe.wait_ge(z1_ready, o.t + 1)
                pe.wait_ge(c_kept, o.t + 1)
                for k in range(KT):
                    last = nc.tensor.transpose(p_a1[:, P * k:P * k + P], z1[:, P * k:P * k + P], idn)
                last.then_inc(z1t_ready, 1)

            def project_z1(o):
                if first(o):
                    pe.wait_ge(w2_ready, 1)
                pe.wait_ge(z1t_kept, o.t + 1)
                pe.wait_ge(h0_kept, o.t + 1)
                for k in range(KT):
                    last = mm(p_a0[:, 0:PW], z1t[:, k, :], w2[:, k, :], start=(k == 0), stop=(k == KT - 1))
                last.then_inc(pj_ready, 1)

            def turn_unit(o):
                pe.wait_ge(un_ready, o.t + 1)
                pe.wait_ge(z1t_kept, o.t + 1)
                settle(pe)
                nc.tensor.transpose(p_a1[0:SH, 0:P], un[:, :], idn).then_inc(unt_ready, 1)

            def angles(o):
                pe.wait_ge(unt_kept, o.t + 1)
                settle(pe)
                mm(p_a1[0:RF, P:2 * P], om[:, :], unt[:, :], start=True, stop=True).then_inc(an_ready, 1)

            def powers(o):
                if first(o):
                    pe.wait_ge(wc_ready, 1)
                pe.wait_ge(ft_ready, o.t + 1)
                after(pe, h1_ready, o.t)
                mm(p_m1[:, 0:(ORDER + 1) * CD], ft[:, :], wc[:, :, :].rearrange("p m c -> p (m c)"),
                   start=True, stop=True).then_inc(y_ready, 1)

            def turn_phi(o):
                pe.wait_ge(phi_steps, ORDER * (o.t + 1))
                after(pe, z2l_ready, o.t)
                settle(pe)
                nc.tensor.transpose(p_m0[0:CD, 0:P], ho[:, ORDER - 1, :], idn).then_inc(pht_ready, 1)

            def gram(o):
                pe.wait_ge(pht_kept, o.t + 1)
                pe.wait_ge(y_kept, o.t + 1)
                mm(p_m1[:, 0:P], pht[:, :], pht[:, :], start=True, stop=True).then_inc(gram_ready, 1)

            def turn_weights(o):
                pe.wait_ge(at_ready, o.t + 1)
                pe.wait_ge(pht_kept, o.t + 1)
                nc.tensor.transpose(p_m0[:, 0:P], at[:, :], idn).then_inc(att_ready, 1)

            def mix(o):
                pe.wait_ge(att_kept, o.t + 1)
                pe.wait_ge(lg_ready, o.t + 1)
                mm(p_m1[:, 0:E], att[:, :], pj[o.par][:, 0:E], start=True, stop=True).then_inc(mixed_ready, 1)

            def turn_z2(o):
                pe.wait_ge(z2_ready, o.t + 1)
                pe.wait_ge(att_kept, o.t + 1)
                for k in range(KT):
                    last = nc.tensor.transpose(p_m0[:, P * k:P * k + P], z2[:, P * k:P * k + P], idn)
                last.then_inc(z2t_ready, 1)

            def widen(o, j):
                if j == 0:
                    if first(o):
                        pe.wait_ge(ffn_ready, 2)
                    pe.wait_ge(z2l_ready, o.t + 1)
                    after(pe, res_ready, o.t)
                else:
                    if first(o):
                        pe.wait_ge(b3_ready, 1)
                    after(pe, glo_ready, 2 * o.t)
                for k in range(KT):
                    for n, half in enumerate((z2h, z2l)):
                        last = mm(p_f[:, j, :], half[:, k, :], fc[:, k, 512 * j:512 * j + 512],
                                  start=(k == 0 and n == 0), stop=(k == KT - 1 and n == 1))
                last.then_inc(fc_ready, 1)

            def turn_hidden(o, j):
                if j == 0:
                    pe.wait_ge(gn_ready, o.t + 1)
                for m in range(4 * j, 4 * j + 4):
                    last = nc.tensor.transpose(p_f[:, j, P * (m % 4):P * (m % 4) + P], gn[:, P * m:P * m + P], idn)
                last.then_inc(gt_ready, 1)

            def narrow(o, j):
                pe.wait_ge(glo_ready, 2 * o.t + j + 1)
                for m in range(4 * j, 4 * j + 4):
                    for n, half in enumerate((gh, glo)):
                        last = mm(p_f[:, 0, 0:E], half[:, m, :], pr[:, m, :],
                                  start=(m == 0 and n == 0), stop=(m == HC - 1 and n == 1))
                if j == 1:
                    last.then_inc(ff_ready, 1)

            def merge_weights():
                pe.wait_ge(in_pack, 16)
                pe.wait_ge(bvw_ready, 1)
                for n in range(KT):
                    for k in range(KT):
                        mm(p_m0[:, E * n:E * n + E], mv[:, k, P * n:P * n + P], mo[:, k, :], start=(k == 0), stop=(k == KT - 1))
                for k in range(KT):
                    last = mm(p_m1[:, 0:E], bvw[:, k, :], mo[:, k, :], start=(k == 0), stop=(k == KT - 1))
                last.then_inc(w2_made, 1)

            def total_magnitudes():
                pe.wait_ge(abs_summed, 2)
                pe.wait_ge(ones_set, 1)
                mm(p_f[:, 0, 0:2], ones[:, :], absum[:, :], start=True, stop=True).then_inc(abs_total, 1)

            def narrow_bias():
                pe.wait_ge(lnbw_ready, 1)
                pe.wait_ge(ffn_ready, 2)
                for m in range(HC):
                    last = mm(p_f[:, 1, 0:E], lnbw[:, m, :], pr[:, m, :].bitcast(F32), start=(m == 0), stop=(m == HC - 1))
                last.then_inc(b3_made, 1)

            def step(do, once):
                do(project_qv, 0, 0)
                do(project_qv, 0, 1)
                do(widen, 3, 0)
                do(widen, 3, 1)
                do(turn_z1, 1)
                do(project_k, 0, 0)
                do(turn_phi, 2)
                do(project_z1, 1)
                once(total_magnitudes, 1)
                do(project_k, 0, 1)
                do(gram, 2)
                do(scores, 0)
                do(turn_unit, 1)
                once(merge_weights, 0)
                do(turn_hidden, 3, 0)
                do(angles, 1)
                do(turn_hidden, 3, 1)
                once(narrow_bias, 1)
                do(turn_weights, 2)
                do(mix, 2)
                do(narrow, 3, 0)
                do(context, 0)
                do(narrow, 3, 1)
                do(powers, 1)
                do(turn_z2, 2)
                do(join_heads, 0)

            pe.wait_ge(in_qkv, 32)
            steps(pe, step)

        @block.vector
        def _(dve):
            v = nc.vector
            dve.wait_ge(in_qkv, 32)
            v.tensor_scalar(bqm[:, :], col[:, COL_MASK:COL_MASK + HH], col[:, COL_BQ:COL_BQ + 1], None,
                            ALU.mult).then_inc(bqm_ready, 1)

            def constants():
                dve.wait_ge(in_pack, 16)
                v.tensor_copy(w2[:, :, E:PW], part("m_shell").rearrange("p (k c) -> p k c", k=KT))
                v.tensor_copy(b2[:, E:PW], part("b_shell"))
                v.tensor_scalar(tmp[:, 4:5], part("temp"), 0.0, 0.1, ALU.max, ALU.add).then_inc(temp_dve, 1)
                dve.wait_ge(temp_dve, 1)
                dve.wait_ge(temp_act, 3)
                v.tensor_tensor(tmp[:, 5:6], tmp[:, 4:5], tmp[:, 3:4], ALU.add).then_inc(temp_dve, 1)
                dve.wait_ge(temp_dve, 2)
                v.reciprocal(tmp[:, 6:7], tmp[:, 5:6]).then_inc(temp_dve, 1)
                dve.wait_ge(temp_dve, 3)
                v.tensor_scalar(dec[:, :], part("decay"), tmp[:, 6:7], None, ALU.mult).then_inc(dec_ready, 1)

            def merged_bias():
                dve.wait_ge(w2_made, 1)
                v.tensor_copy(w2[:, :, 0:E], p_m0[:, :].rearrange("p (n e) -> p n e", n=KT))
                v.tensor_tensor(b2[:, 0:E], p_m1[:, 0:E], part("b_out"), ALU.add).then_inc(w2_ready, 1)

            def scaled_features():
                dve.wait_ge(in_feat, 32)
                for m in range(ORDER + 1):
                    last = v.tensor_scalar(wc[:, m, :], wc_raw[:, m, :], MAGS[m] * RFF_SCALE, None, ALU.mult)
                last.then_inc(wc_ready, 1)

            def keep_bias3():
                dve.wait_ge(b3_made, 1)
                v.tensor_copy(b3[:, :], p_f[:, 1, 0:E]).then_inc(b3_ready, 1)

            def ternary():
                dve.wait_ge(abs_total, 1)
                v.tensor_scalar(thr[:, 0:2], p_f[:, 0, 0:2], 0.5 / (E * HID), 0.5e-6, ALU.mult, ALU.add).then_inc(thr_steps, 1)
                dve.wait_ge(thr_steps, 1)
                v.tensor_scalar(thr[:, 2:4], thr[:, 0:2], -1.0, None, ALU.mult).then_inc(thr_steps, 1)
                dve.wait_ge(thr_steps, 2)
                for n, (raw, cut) in enumerate(((fc_raw, fc), (pr_raw, pr))):
                    flat = raw[:, :, :].rearrange("p a b -> p (a b)")
                    if n:
                        dve.wait_ge(ffn_ready, n)
                    v.tensor_scalar(below[:, :], flat, thr[:, 2 + n:3 + n], None, ALU.is_lt).then_inc(below_ready, 1)
                    dve.wait_ge(below_ready, n + 1)
                    v.scalar_tensor_tensor(cut[:, :, :].rearrange("p a b -> p (a b)"), flat, thr[:, n:n + 1], below[:, :],
                                           ALU.is_gt, ALU.subtract).then_inc(ffn_ready, 1)

            def turn_v(o):
                dve.wait_ge(qv_ready, o.t + 1)
                v.transpose(qt[:, :, :, :].rearrange("p b l e -> p l b e"),
                            p_qv[:, :].rearrange("p (l b e) -> p l b e", l=HL, b=TB)).then_inc(v_turned, 1)
                dve.wait_ge(v_turned, o.t + 1)
                after(dve, c_ready, o.t)
                vs = qt[:, :, :, :].rearrange("p b l e -> p b (l e)")[:, :, D:3 * D].rearrange("p b (l d) -> p b l d", l=HL)
                for h in range(HH):
                    last = v.tensor_scalar(vm[:, :, h, :].rearrange("p (b l) d -> p b l d", l=HL), vs,
                                           col[:, COL_MASK + h:COL_MASK + h + 1], None, ALU.mult)
                last.then_inc(v_masked, 1)

            def less_max(o):
                dve.wait_ge(s_ready, o.t + 1)
                grouped = p_a0[:, 0:C].rearrange("p (g n) -> p g n", g=G)
                v.tensor_reduce(smax[:, :], grouped, AX.X, ALU.max).then_inc(s_max, 1)
                dve.wait_ge(s_max, o.t + 1)
                after(dve, s_exp, o.t)
                v.tensor_tensor(sc[:, :, :], grouped, smax[:, :].unsqueeze(2).to_broadcast([P, G, N]),
                                ALU.subtract).then_inc(s_less, 1)

            def probabilities(o):
                dve.wait_ge(s_exp, o.t + 1)
                v.tensor_reduce(ssum[:, :], pe_[:, :, :], AX.X, ALU.add).then_inc(s_sum, 1)
                dve.wait_ge(s_sum, o.t + 1)
                v.reciprocal(srec[:, :], ssum[:, :]).then_inc(s_rec, 1)
                dve.wait_ge(s_rec, o.t + 1)
                v.tensor_tensor(pn[:, :, :], pe_[:, :, :], srec[:, :].unsqueeze(2).to_broadcast([P, G, N]),
                                ALU.mult).then_inc(p_ready, 1)
                dve.wait_ge(p_ready, o.t + 1)
                after(dve, c_ready, o.t)
                v.transpose(pt[:, :, :].rearrange("p g n -> p (g n)"),
                            pn[:, :, :].rearrange("p g n -> p (g n)")).then_inc(p_turned, 1)

            def keep_h0(o):
                dve.wait_ge(h0_ready, o.t + 1)
                after(dve, h1_ready, o.t - 1)
                v.tensor_tensor(h0[o.par][:, :], p_a0[:, 0:E], bo, ALU.add).then_inc(h0_kept, 1)
                dve.wait_ge(h0_kept, o.t + 1)
                v.bn_stats(st1[:, :], h0[o.par][:, :]).then_inc(st1_ready, 1)
                dve.wait_ge(st1_ready, o.t + 1)
                after(dve, var1_ready, o.t)
                settle(dve)
                v.bn_aggr(mv1[:, :], st1[:, :]).then_inc(mv1_ready, 1)

            def center1(o):
                dve.wait_ge(mv1_ready, o.t + 1)
                after(dve, z1t_ready, o.t)
                v.tensor_scalar(z1[:, :], h0[o.par][:, :], mv1[:, 0:1], None, ALU.subtract).then_inc(z1_ready, 1)

            def keep_projection(o):
                if first(o):
                    dve.wait_ge(w2_ready, 1)
                dve.wait_ge(pj_ready, o.t + 1)
                after(dve, mixed_ready, o.t - 1)
                after(dve, charge_ready, o.t - 1)
                dve.wait_ge(rs1_ready, o.t + 1)
                v.scalar_tensor_tensor(pj[o.par][:, :], p_a0[:, 0:PW], rs1[:, 1:2], b2[:, :], ALU.mult,
                                       ALU.add).then_inc(pj_kept, 1)
                dve.wait_ge(pj_kept, o.t + 1)
                after(dve, floor_ready, o.t)
                shell = pj[o.par][:, E:E + SH]
                v.tensor_tensor_reduce(sq[:, :], shell, shell, 1.0, 0.0, ALU.mult, ALU.add, nn[:, 0:1]).then_inc(n2_ready, 1)

            def unit(o):
                dve.wait_ge(rn_ready, o.t + 1)
                after(dve, unt_ready, o.t)
                v.tensor_scalar(un[:, :], pj[o.par][:, E:E + SH], nn[:, 2:3], None, ALU.mult).then_inc(un_ready, 1)

            def reduce_angles(o):
                dve.wait_ge(an_ready, o.t + 1)
                n = 6 * o.t
                v.tensor_scalar(ang[:, 0, :], p_a1[0:RF, P:2 * P], col[0:RF, COL_RB:COL_RB + 1], None,
                                ALU.add).then_inc(an_steps, 1)
                dve.wait_ge(an_steps, n + 1)
                v.tensor_scalar(ang[:, 1, :], ang[:, 0, :], 0.5 / math.pi, col[0:RF, COL_OFF:COL_OFF + 1], ALU.mult,
                                ALU.add).then_inc(an_steps, 1)
                dve.wait_ge(an_steps, n + 2)
                v.tensor_scalar(ang[:, 2, :], ang[:, 1, :], MAGIC, MAGIC, ALU.add, ALU.subtract).then_inc(an_steps, 1)
                dve.wait_ge(an_steps, n + 3)
                v.scalar_tensor_tensor(ang[:, 3, :], ang[:, 2, :], -TWO_PI_HI, ang[:, 0, :], ALU.mult,
                                       ALU.add).then_inc(an_steps, 1)
                dve.wait_ge(an_steps, n + 4)
                v.scalar_tensor_tensor(ang[:, 1, :], ang[:, 2, :], -TWO_PI_LO, ang[:, 3, :], ALU.mult,
                                       ALU.add).then_inc(an_steps, 1)
                dve.wait_ge(an_steps, n + 5)
                after(dve, ft_ready, o.t)
                v.tensor_scalar(ang[:, 4, :], ang[:, 1, :], col[0:RF, COL_HI:COL_HI + 1], col[0:RF, COL_LO:COL_LO + 1],
                                ALU.min, ALU.max).then_inc(an_steps, 1)

            def combine(o):
                dve.wait_ge(y_kept, o.t + 1)
                dve.wait_ge(charge_ready, o.t + 1)
                after(dve, pht_ready, o.t)
                for m in range(ORDER):
                    src = yy[:, ORDER, :] if m == 0 else ho[:, m - 1, :]
                    if m:
                        dve.wait_ge(phi_steps, ORDER * o.t + m)
                    v.scalar_tensor_tensor(ho[:, m, :], src, qc[o.par][:, :], yy[:, ORDER - 1 - m, :], ALU.mult,
                                           ALU.add).then_inc(phi_steps, 1)

            def logits(o):
                if first(o):
                    dve.wait_ge(dec_ready, 1)
                dve.wait_ge(gram_ready, o.t + 1)
                after(dve, at_ready, o.t)
                v.tensor_tensor(lg[:, 0, :], p_m1[:, 0:P], dec[:, :], ALU.mult).then_inc(lg_ready, 1)
                dve.wait_ge(lg_ready, o.t + 1)
                settle(dve)
                v.tensor_tensor_reduce(lg[:, 1, :], lg[:, 0, :], hid, -1.0, 3e38, ALU.add, ALU.min,
                                       nmx[:, :]).then_inc(lg_max, 1)

            def residual(o):
                dve.wait_ge(at_ready, o.t + 1)
                v.reciprocal(asum[:, 1:2], asum[:, 0:1]).then_inc(arec_ready, 1)
                dve.wait_ge(mixed_ready, o.t + 1)
                dve.wait_ge(arec_ready, o.t + 1)
                after(dve, res_ready, o.t - 1)
                v.scalar_tensor_tensor(h1[o.par][:, :], p_m1[:, 0:E], asum[:, 1:2], h0[o.par][:, :], ALU.mult,
                                       ALU.add).then_inc(h1_ready, 1)
                dve.wait_ge(h1_ready, o.t + 1)
                v.bn_stats(st2[:, :], h1[o.par][:, :]).then_inc(st2_ready, 1)
                dve.wait_ge(st2_ready, o.t + 1)
                after(dve, var2_ready, o.t)
                settle(dve)
                v.bn_aggr(mv2[:, :], st2[:, :]).then_inc(mv2_ready, 1)

            def center2(o):
                dve.wait_ge(mv2_ready, o.t + 1)
                after(dve, z2t_ready, o.t)
                v.tensor_scalar(z2[:, :], h1[o.par][:, :], mv2[:, 0:1], None, ALU.subtract).then_inc(z2_ready, 1)

            def low_z2(o):
                dve.wait_ge(z2h_ready, o.t + 1)
                after(dve, fc_ready, 2 * o.t)
                v.tensor_tensor(z2l[:, :, :], p_m0[:, 0:E].rearrange("p (k n) -> p k n", k=KT), z2h[:, :, :].bitcast(F32),
                                ALU.subtract).then_inc(z2l_ready, 1)

            def stats3(o, j):
                dve.wait_ge(gl_ready, 2 * o.t + j + 1)
                v.bn_stats(st3[:, 6 * j:6 * j + 6], gl[:, 512 * j:512 * j + 512]).then_inc(st3_ready, 1)
                if j:
                    dve.wait_ge(st3_ready, 2 * o.t + 2)
                    after(dve, var3_ready, o.t)
                    settle(dve)
                    v.bn_aggr(mv3[:, :], st3[:, :]).then_inc(mv3_ready, 1)

            def center3(o):
                dve.wait_ge(mv3_ready, o.t + 1)
                if first(o):
                    dve.wait_ge(in_ffn, 48)
                after(dve, gt_ready, 2 * o.t)
                v.scalar_tensor_tensor(gn[:, :], gl[:, :], mv3[:, 0:1], lnw[:, :], ALU.subtract, ALU.mult).then_inc(gn_ready, 1)

            def low_hidden(o, j):
                dve.wait_ge(gh_ready, 2 * o.t + j + 1)
                after(dve, ff_ready, o.t)
                v.tensor_tensor(glo[:, 4 * j:4 * j + 4, :], p_f[:, j, :].rearrange("p (m n) -> p m n", n=P),
                                gh[:, 4 * j:4 * j + 4, :].bitcast(F32), ALU.subtract).then_inc(glo_ready, 1)

            def result(o):
                dve.wait_ge(ff_ready, o.t + 1)
                dve.wait_ge(rs3_ready, o.t + 1)
                dve.wait_ge(h1_biased, o.t + 1)
                after(dve, stored, 16 * o.t)
                v.scalar_tensor_tensor(res[:, :], p_f[:, 0, 0:E], rs3[:, 1:2], h1[o.par][:, :], ALU.mult,
                                       ALU.add).then_inc(res_ready, 1)

            def step(do, once):
                do(center1, 1)
                once(constants, 1)
                once(merged_bias, 1)
                do(combine, 2)
                do(turn_v, 0)
                do(stats3, 3, 0)
                do(stats3, 3, 1)
                do(keep_projection, 1)
                do(center3, 3)
                once(scaled_features, 0)
                once(ternary, 1)
                do(unit, 1)
                do(logits, 2)
                do(less_max, 0)
                do(reduce_angles, 1)
                do(low_hidden, 3, 0)
                do(probabilities, 0)
                do(low_hidden, 3, 1)
                do(residual, 2)
                do(center2, 2)
                do(result, 3)
                once(keep_bias3, 2)
                do(low_z2, 2)
                do(keep_h0, 0)

            steps(dve, step)


def kernel(**inputs):
    import numpy as np
    import concourse.bacc as bacc
    from concourse.bass_utils import run_bass_kernel_spmd as run

    def take(name):
        return np.asarray(inputs[name])

    nc = bacc.Bacc("TRN2", target_bir_lowering=False, num_devices=1)
    f4 = np.float32
    x = take("x").reshape(TILES, TB, N, HQ, HM, HL, KT, P).transpose(0, 7, 5, 6, 3, 1, 4, 2).reshape(TILES, P, HL, KT, HQ, C)

    def by_k(w):
        return w.T.reshape(w.shape[1] // P, P, w.shape[0]).transpose(1, 0, 2)

    wq, wk, wv = [by_k(take(f"L0_tok_W{n}")) for n in "qkv"]
    none = np.zeros_like(wk)
    pairs = [[(wq, wv), (wv, wq)], [(wk, none), (none, wk)]]
    qkv = np.stack([np.stack([np.concatenate(p, axis=2) for p in row], axis=2) for row in pairs], axis=1)
    wo = take("L0_tok_Wo").T.reshape(HQ, HM, HL, D, E).transpose(0, 1, 3, 2, 4).reshape(P, HL, E)
    rows = lambda v: np.broadcast_to(v.reshape(1, -1), (P, v.size))

    cols = np.zeros((P, COLS), f4)
    cols[:, COL_MASK:COL_MASK + HH] = (np.arange(P)[:, None] // D) % HH == np.arange(HH)
    for c, n in ((COL_BQ, "q"), (COL_BK, "k"), (COL_BV, "v")):
        cols[:, c] = np.tile(take(f"L0_tok_b{n}"), P // D)
    cols[:RF, COL_RB] = np.tile(take("L0_attn_rff_bias"), 2)
    cosine = np.arange(RF) < RF // 2
    cols[:RF, COL_OFF] = np.where(cosine, 0.25, 0.0)
    cols[:RF, COL_SHIFT] = np.where(cosine, HALF_PI, 0.0)
    cols[:RF, COL_HI] = np.where(cosine, PI_IN - HALF_PI, PI_IN)
    cols[:RF, COL_LO] = np.where(cosine, -PI_IN - HALF_PI, -PI_IN)
    cols[:, COL_MBV:COL_MBV + KT] = take("L0_attn_b_v").reshape(KT, P).T
    cols[:, COL_LNB:COL_LNB + HC] = take("L0_ffn_ln_b").reshape(HC, P).T

    tok = np.arange(P)
    seen = (tok[:, None] // N == tok[None, :] // N) & (tok[:, None] >= tok[None, :])
    decay = np.where(seen, np.exp(-0.3 * np.abs(tok[:, None] - tok[None, :]) / 10.0), 0.0).astype(f4)
    hidden = np.where(seen, 0.0, -1e30).astype(f4)

    w_v = take("L0_attn_W_v").reshape(KT, P, E).transpose(1, 0, 2)
    comb = take("L0_attn_W_combine").reshape(CD, ORDER + 1, RF).transpose(2, 1, 0)
    omega = np.tile(take("L0_attn_omega").T, (1, 2))
    parts = {
        "ident": np.eye(P, dtype=f4), "w_o": wo, "b_o": rows(take("L0_tok_bo")), "m_out": by_k(take("L0_attn_W_out")),
        "m_v": w_v, "m_shell": by_k(np.concatenate([take("L0_attn_W_shell"), take("L0_attn_W_charge")])),
        "b_out": rows(take("L0_attn_b_out")),
        "b_shell": rows(np.concatenate([take("L0_attn_b_shell"), take("L0_attn_b_charge")])),
        "temp": rows(take("L0_attn_log_temp")), "decay": decay, "hidden": hidden,
    }
    packed = np.concatenate([parts[n].reshape(P, -1) for n in PACK], axis=1)
    arrays = {
        "x": x, "cols": cols, "w_qkv": qkv, "packed": packed, "omega": omega, "w_comb": comb,
        "w_fc": by_k(take("L0_ffn_W_fc")), "w_proj": by_k(take("L0_ffn_W_proj")), "ln_w": rows(take("L0_ffn_ln_w")),
    }
    arrays = {f"in_{n}": np.ascontiguousarray(a) for n, a in arrays.items()}
    args = [nc.dram_tensor(n, a.shape, mybir.dt.from_np(a.dtype), kind="ExternalInput").ap() for n, a in arrays.items()]
    out = nc.dram_tensor("out_0", (TILES, P, E), F32, kind="ExternalOutput").ap()
    audio_tower(nc, *args, out)
    r = run(nc, [arrays], core_ids=[0])
    return r.results[0]["out_0"].reshape(B, N, E)
```

```python
from collections import namedtuple
from contextlib import ExitStack
import math

import concourse.bass as bass
from concourse import mybir

F32 = mybir.dt.float32
FR = mybir.dt.float32r
ALU = mybir.AluOpType
ACT = mybir.ActivationFunctionType
AX = mybir.AxisListType

P = 128
E = 256
KT = E // P
B, S = 64, 256
H, D = 16, 16
N = S // H
HQ, HM, HL = 4, 2, 2
QP = P // HQ
HH = QP // N
TILES = 8
LAGS = 3
TB = B // TILES
G = TB * HM
C = G * N
SH = 64
RF = 64
CD = 64
PARTS = 4
ORDER = 4
HID = 1024
HC = HID // P
PW = E + SH + 1
EPS = 1e-5
TINY = 1e-24
MAGIC = 1.5 * 2.0 ** 23
TWO_PI_HI = 6.28125
TWO_PI_LO = 2.0 * math.pi - TWO_PI_HI
HALF_PI = 0.5 * math.pi
PI_IN = 3.141592
RFF_SCALE = math.sqrt(2.0 / RF) * math.sqrt(math.exp(-0.5))
MAGS = [math.sqrt(1.0 / math.factorial(m) + 1e-10) for m in range(ORDER + 1)]

COL_MASK = 0
COL_BQ, COL_BK, COL_BV = HH, HH + 1, HH + 2
COL_RB = HH + 3
COL_OFF = HH + 4
COL_SHIFT = HH + 5
COL_HI, COL_LO = HH + 6, HH + 7
COL_MBV = HH + 8
COL_LNB = COL_MBV + KT
COLS = COL_LNB + HC

PACK = {}
PACKED = 0
for _name, _width in (("ident", P), ("w_o", HL * E), ("b_o", E), ("m_out", KT * E), ("m_v", KT * E),
                      ("m_shell", KT * (SH + 1)), ("b_out", E), ("b_shell", SH + 1), ("temp", 1),
                      ("decay", P), ("hidden", P)):
    PACK[_name] = (PACKED, PACKED + _width)
    PACKED += _width

Tile = namedtuple("Tile", "t par pair")


def first(o):
    return isinstance(o.t, int) and o.t == 0


def after(eng, sem, count):
    if not (isinstance(count, int) and count <= 0):
        eng.wait_ge(sem, count)


def settle(eng):
    eng.nop(nofuse=True)


def steps(eng, step, loop_from=4):
    def run(i, n):
        def do(operation, lag, *which):
            k = n - lag
            if isinstance(i, int):
                if 0 <= k < TILES:
                    operation(Tile(k, k % 2, k // 2), *which)
            else:
                operation(Tile(2 * i + k, k % 2, i + k // 2), *which)

        def once(setup, at, *which):
            if isinstance(i, int) and n == at:
                setup(*which)
        step(do, once)

    for s in range(loop_from):
        run(0, s)
    with eng.Fori(0, 2) as i:
        run(i, loop_from)
        run(i, loop_from + 1)
    for s in range(loop_from + 4, TILES + LAGS):
        run(0, s)


def audio_tower(nc, x, cols, w_qkv, packed, omega, w_comb, w_fc, w_proj, ln_w, out):
    with ExitStack() as ctx:
        def sb(name, shape, dt=F32):
            return ctx.enter_context(nc.sbuf_tensor(name, shape, dt))

        def sem(name):
            return ctx.enter_context(nc.semaphore(name))

        col = sb("col", [P, COLS])
        wq = sb("wq", [P, 2, KT, HL, 2 * D])
        bqm = sb("bqm", [P, HH])
        pk = sb("pk", [P, PACKED])
        bvw = sb("bvw", [P, KT, P])
        w2 = sb("w2", [P, KT, PW])
        b2 = sb("b2", [P, PW])
        om = sb("om", [SH, RF])
        wc_raw = sb("wc_raw", [RF, ORDER + 1, CD])
        wc = sb("wc", [RF, ORDER + 1, CD])
        fc_raw = sb("fc_raw", [P, KT, HID])
        pr_raw = sb("pr_raw", [P, HC, E])
        below = sb("below", [P, 2048])
        fc = sb("fc", [P, KT, HID], FR)
        pr = sb("pr", [P, HC, E], FR)
        absum = sb("absum", [P, 2])
        thr = sb("thr", [P, 4])
        lnw = sb("lnw", [P, HID])
        lnbw = sb("lnbw", [P, HC, P])
        b3 = sb("b3", [P, E])
        ones = sb("ones", [P, P])
        dec = sb("dec", [P, P])
        tmp = sb("tmp", [P, 8])
        mhalf = sb("mhalf", [P, 1])

        def part(name):
            return pk[:, PACK[name][0]:PACK[name][1]]

        idn, bo, hid = part("ident"), part("b_o"), part("hidden")
        wo = part("w_o").rearrange("p (l e) -> p l e", l=HL)
        mo = part("m_out").rearrange("p (k e) -> p k e", k=KT)
        mv = part("m_v").rearrange("p (k e) -> p k e", k=KT)

        raws, cuts = (fc_raw, pr_raw), (fc, pr)

        xt = [sb(f"xt{i}", [P, HL, KT, HQ, C]) for i in range(2)]
        qm = sb("qm", [P, G, HH, N])
        ks = sb("ks", [P, G, N])
        qt = sb("qt", [P, TB, HL, 2 * D])
        vm = sb("vm", [P, G, HH, D])
        smax = sb("smax", [P, G])
        sc = sb("sc", [P, G, N])
        pe_ = sb("pe_", [P, G, N])
        ssum = sb("ssum", [P, G])
        srec = sb("srec", [P, G])
        pn = sb("pn", [P, G, N])
        pt = sb("pt", [P, G, N])
        cx = sb("cx", [P, HL, TB, N])
        h0 = [sb(f"h0_{i}", [P, E]) for i in range(2)]
        st1 = sb("st1", [P, 6])
        mv1 = sb("mv1", [P, 2])
        rs1 = sb("rs1", [P, 2])
        z1 = sb("z1", [P, E])
        z1t = sb("z1t", [P, KT, P])
        pj = [sb(f"pj{i}", [P, PW]) for i in range(2)]
        qc = [sb(f"qc{i}", [P, 1]) for i in range(2)]
        sq = sb("sq", [P, SH])
        nn = sb("nn", [P, 3])
        un = sb("un", [P, SH])
        unt = sb("unt", [SH, P])
        ang = sb("ang", [RF, 5, P])
        ft = sb("ft", [RF, P])
        yy = sb("yy", [P, ORDER + 1, CD])
        ho = sb("ho", [P, ORDER, CD])
        pht = sb("pht", [CD, P])
        lg = sb("lg", [P, 2, P])
        nmx = sb("nmx", [P, 1])
        at = sb("at", [P, P])
        asum = sb("asum", [P, 2])
        att = sb("att", [P, P])
        h1 = [sb(f"h1_{i}", [P, E]) for i in range(2)]
        st2 = sb("st2", [P, 6])
        mv2 = sb("mv2", [P, 2])
        rs2 = [sb(f"rs2_{i}", [P, 2]) for i in range(2)]
        z2 = sb("z2", [P, E])
        z2h = sb("z2h", [P, KT, P], FR)
        z2l = sb("z2l", [P, KT, P], FR)
        gl = sb("gl", [P, HID])
        st3 = sb("st3", [P, 12])
        mv3 = sb("mv3", [P, 2])
        rs3 = sb("rs3", [P, 2])
        gn = sb("gn", [P, HID])
        gh = sb("gh", [P, HC, P], FR)
        glo = sb("glo", [P, HC, P], FR)
        res = sb("res", [P, E])

        def bank(name):
            return ctx.enter_context(nc.psum_tensor(name, [P, 512], F32))

        p_qv, p_k, p_a0, p_a1, p_m0, p_m1 = [bank(n) for n in ("p_qv", "p_k", "p_a0", "p_a1", "p_m0", "p_m1")]
        p_f = ctx.enter_context(nc.psum_tensor("p_f", [P, 2, 512], F32))

        x_in = [[sem(f"x_in{i}{j}") for j in range(HL)] for i in range(2)]
        in_qkv, in_pack, in_feat, in_lnw = sem("in_qkv"), sem("in_pack"), sem("in_feat"), sem("in_lnw")
        in_tern = [sem(f"in_tern{i}") for i in range(2)]
        bqm_ready, half_set, ones_set = sem("bqm_ready"), sem("half_set"), sem("ones_set")
        temp_act, temp_dve, dec_ready, wc_ready = sem("temp_act"), sem("temp_dve"), sem("dec_ready"), sem("wc_ready")
        bvw_ready, w2_made, w2_ready = sem("bvw_ready"), sem("w2_made"), sem("w2_ready")
        abs_summed, abs_total, thr_steps, below_ready, cut_ready = [
            [sem(f"{n}{i}") for i in range(2)] for n in ("abs_summed", "abs_total", "thr_steps", "below_ready", "cut_ready")]
        lnbw_ready, b3_made, b3_ready = sem("lnbw_ready"), sem("b3_made"), sem("b3_ready")
        qv_ready, k_ready, q_kept, k_kept = sem("qv_ready"), sem("k_ready"), sem("q_kept"), sem("k_kept")
        v_turned, v_masked = sem("v_turned"), sem("v_masked")
        s_ready, s_max, s_less, s_exp = sem("s_ready"), sem("s_max"), sem("s_less"), sem("s_exp")
        s_sum, s_rec, p_ready, p_turned = sem("s_sum"), sem("s_rec"), sem("p_ready"), sem("p_turned")
        c_ready, c_kept, h0_ready, h0_kept = sem("c_ready"), sem("c_kept"), sem("h0_ready"), sem("h0_kept")
        st1_ready, mv1_ready, var1_ready, rs1_ready = sem("st1_ready"), sem("mv1_ready"), sem("var1_ready"), sem("rs1_ready")
        z1_ready, z1t_ready, z1t_kept = sem("z1_ready"), sem("z1t_ready"), sem("z1t_kept")
        pj_ready, pj_kept, charge_ready = sem("pj_ready"), sem("pj_kept"), sem("charge_ready")
        n2_ready, floor_ready, rn_ready, un_ready = sem("n2_ready"), sem("floor_ready"), sem("rn_ready"), sem("un_ready")
        unt_ready, unt_kept, an_ready, an_steps = sem("unt_ready"), sem("unt_kept"), sem("an_ready"), sem("an_steps")
        ft_ready = sem("ft_ready")
        y_ready, y_kept, phi_steps = sem("y_ready"), sem("y_kept"), sem("phi_steps")
        pht_ready, pht_kept, gram_ready = sem("pht_ready"), sem("pht_kept"), sem("gram_ready")
        lg_ready, lg_max, at_ready, arec_ready = sem("lg_ready"), sem("lg_max"), sem("at_ready"), sem("arec_ready")
        att_ready, att_kept, mixed_ready, h1_ready = sem("att_ready"), sem("att_kept"), sem("mixed_ready"), sem("h1_ready")
        st2_ready, mv2_ready, var2_ready, rs2_ready = sem("st2_ready"), sem("mv2_ready"), sem("var2_ready"), sem("rs2_ready")
        z2_ready, z2t_ready, z2h_ready, z2l_ready = sem("z2_ready"), sem("z2t_ready"), sem("z2h_ready"), sem("z2l_ready")
        fc_ready, gl_ready, st3_ready, mv3_ready = sem("fc_ready"), sem("gl_ready"), sem("st3_ready"), sem("mv3_ready")
        var3_ready, rs3_ready, gn_ready, gt_ready = sem("var3_ready"), sem("rs3_ready"), sem("gn_ready"), sem("gt_ready")
        gh_ready, glo_ready, h1_biased = sem("gh_ready"), sem("glo_ready"), sem("h1_biased")
        ff_ready, res_ready, stored = sem("ff_ready"), sem("res_ready"), sem("stored")

        block = ctx.enter_context(nc.Block())

        @block.sync
        def _(sp):
            def load(o):
                for j in range(HL):
                    after(sp, qv_ready, o.t - 1)
                    after(sp, k_ready, o.t - 1)
                    sp.dma_start(xt[o.par][:, j], x[o.t, :, j]).then_inc(x_in[o.par][j], 16)

            def load_pack():
                sp.dma_start(pk[:, :], packed).then_inc(in_pack, 16)

            def load_features():
                sp.dma_start(om[:, :], omega).then_inc(in_feat, 16)
                sp.dma_start(wc_raw[:, :, :], w_comb).then_inc(in_feat, 16)

            def load_ternary():
                sp.dma_start(fc_raw[:, :, :], w_fc).then_inc(in_tern[0], 16)
                sp.dma_start(pr_raw[:, :, :], w_proj).then_inc(in_tern[1], 16)
                sp.dma_start(lnw[:, :], ln_w).then_inc(in_lnw, 16)

            def store(o):
                sp.wait_ge(res_ready, o.t + 1)
                sp.dma_start(out[o.t], res[:, :]).then_inc(stored, 16)

            def step(do, once):
                once(load_pack, 0)
                do(load, -1)
                once(load_ternary, 0)
                once(load_features, 0)
                do(store, 3)

            sp.dma_start(wq[:, :, :, :, :], w_qkv).then_inc(in_qkv, 16)
            sp.dma_start(col[:, :], cols).then_inc(in_qkv, 16)
            load(Tile(0, 0, 0))
            steps(sp, step, loop_from=3)
            sp.wait_ge(stored, 16 * TILES)

        @block.gpsimd
        def _(pool):
            pool.memset(mhalf[:, :], -0.5).then_inc(half_set, 1)
            pool.memset(ones[:, :], 1.0).then_inc(ones_set, 1)
            pool.wait_ge(half_set, 1)
            pool.wait_ge(ones_set, 1)
            pool.wait_ge(in_qkv, 32)

            def repeat_biases():
                for k in range(KT):
                    last = pool.tensor_scalar(bvw[:, k, :], ones[:, :], col[:, COL_MBV + k:COL_MBV + k + 1], None, ALU.mult)
                last.then_inc(bvw_ready, 1)

            def repeat_inner_bias():
                for m in range(HC):
                    last = pool.tensor_scalar(lnbw[:, m, :], ones[:, :], col[:, COL_LNB + m:COL_LNB + m + 1], None, ALU.mult)
                last.then_inc(lnbw_ready, 1)

            def root1(o):
                pool.wait_ge(mv1_ready, o.t + 1)
                after(pool, pj_kept, o.t)
                settle(pool)
                pool.tensor_scalar(rs1[:, 0:1], mv1[:, 1:2], EPS, None, ALU.add).then_inc(var1_ready, 1)
                pool.wait_ge(var1_ready, o.t + 1)
                pool.tensor_tensor(rs1[:, 1:2], rs1[:, 0:1], mhalf[:, :], ALU.pow).then_inc(rs1_ready, 1)

            def root2(o):
                pool.wait_ge(mv2_ready, o.t + 1)
                after(pool, gl_ready, 2 * (o.t - 1))
                settle(pool)
                rs = rs2[o.par]
                pool.tensor_scalar(rs[:, 0:1], mv2[:, 1:2], EPS, None, ALU.add).then_inc(var2_ready, 1)
                pool.wait_ge(var2_ready, o.t + 1)
                pool.tensor_tensor(rs[:, 1:2], rs[:, 0:1], mhalf[:, :], ALU.pow).then_inc(rs2_ready, 1)

            def bias_residual(o):
                if first(o):
                    pool.wait_ge(b3_ready, 1)
                pool.wait_ge(z2_ready, o.t + 1)
                pool.tensor_tensor(h1[o.par][:, :], h1[o.par][:, :], b3[:, :], ALU.add).then_inc(h1_biased, 1)

            def root_norm(o):
                pool.wait_ge(n2_ready, o.t + 1)
                after(pool, un_ready, o.t)
                settle(pool)
                pool.tensor_scalar(nn[:, 1:2], nn[:, 0:1], TINY, None, ALU.max).then_inc(floor_ready, 1)
                pool.wait_ge(floor_ready, o.t + 1)
                pool.tensor_tensor(nn[:, 2:3], nn[:, 1:2], mhalf[:, :], ALU.pow).then_inc(rn_ready, 1)

            def root3(o):
                pool.wait_ge(mv3_ready, o.t + 1)
                after(pool, res_ready, o.t)
                settle(pool)
                pool.tensor_scalar(rs3[:, 0:1], mv3[:, 1:2], EPS, None, ALU.add).then_inc(var3_ready, 1)
                pool.wait_ge(var3_ready, o.t + 1)
                pool.tensor_tensor(rs3[:, 1:2], rs3[:, 0:1], mhalf[:, :], ALU.pow).then_inc(rs3_ready, 1)

            def step(do, once):
                once(repeat_inner_bias, 0)
                do(root2, 2)
                once(repeat_biases, 0)
                do(bias_residual, 2)
                do(root3, 2)
                do(root1, 0)
                do(root_norm, 0)

            steps(pool, step)

        @block.scalar
        def _(act):
            a = nc.scalar.activation

            def temperature():
                act.wait_ge(in_pack, 16)
                a(tmp[:, 1:2], part("temp"), ACT.Abs).then_inc(temp_act, 1)
                act.wait_ge(temp_act, 1)
                a(tmp[:, 2:3], tmp[:, 1:2], ACT.Exp, scale=-1.0).then_inc(temp_act, 1)
                act.wait_ge(temp_act, 2)
                a(tmp[:, 3:4], tmp[:, 2:3], ACT.Ln, bias=1.0).then_inc(temp_act, 1)

            def magnitudes(n):
                act.wait_ge(in_tern[n], 16)
                a(cuts[n][:, :, :], raws[n][:, :, :], ACT.Abs, accum_out=absum[:, n:n + 1]).then_inc(abs_summed[n], 1)

            def keep_q(o):
                act.wait_ge(v_turned, o.t + 1)
                after(act, s_ready, o.t)
                if first(o):
                    act.wait_ge(bqm_ready, 1)
                for h in range(HH):
                    last = a(qm[:, :, h, :], p_qv[:, C * h:C * h + C].rearrange("p (g n) -> p g n", g=G), ACT.Identity,
                             bias=bqm[:, h:h + 1], scale=col[:, COL_MASK + h:COL_MASK + h + 1])
                last.then_inc(q_kept, 1)

            def keep_k(o):
                act.wait_ge(k_ready, o.t + 1)
                after(act, s_ready, o.t)
                a(ks[:, :, :], p_k[:, 0:C].rearrange("p (g n) -> p g n", g=G), ACT.Identity,
                  bias=col[:, COL_BK:COL_BK + 1]).then_inc(k_kept, 1)

            def exp_scores(o):
                act.wait_ge(s_less, o.t + 1)
                after(act, p_ready, o.t)
                a(pe_[:, :, :], sc[:, :, :], ACT.Exp, scale=D ** -0.5).then_inc(s_exp, 1)

            def keep_context(o):
                act.wait_ge(c_ready, o.t + 1)
                after(act, h0_ready, o.t)
                a(cx[:, :, :, :], p_a1[:, 0:C].rearrange("p (b l i) -> p l b i", b=TB, l=HL), ACT.Identity,
                  bias=col[:, COL_BV:COL_BV + 1]).then_inc(c_kept, 1)

            def keep_z1(o):
                act.wait_ge(z1t_ready, o.t + 1)
                after(act, pj_ready, o.t)
                a(z1t[:, :, :], p_a1[:, 0:E].rearrange("p (k n) -> p k n", k=KT), ACT.Copy).then_inc(z1t_kept, 1)

            def charge(o):
                act.wait_ge(pj_kept, o.t + 1)
                after(act, phi_steps, ORDER * (o.t - 1))
                a(qc[o.par][:, :], pj[o.par][:, PW - 1:PW], ACT.Tanh).then_inc(charge_ready, 1)

            def keep_unit(o):
                act.wait_ge(unt_ready, o.t + 1)
                after(act, an_ready, o.t)
                a(unt[:, :], p_a1[0:SH, 0:P], ACT.Copy).then_inc(unt_kept, 1)

            def sines(o):
                act.wait_ge(an_steps, 6 * o.t + 6)
                after(act, y_ready, o.t)
                a(ft[:, :], ang[:, 4, :], ACT.Sin, bias=col[0:RF, COL_SHIFT:COL_SHIFT + 1]).then_inc(ft_ready, 1)

            def keep_powers(o):
                act.wait_ge(y_ready, o.t + 1)
                after(act, phi_steps, ORDER * o.t)
                a(yy[:, :, :], p_m1[:, 0:(ORDER + 1) * CD], ACT.Copy).then_inc(y_kept, 1)

            def keep_phi(o):
                act.wait_ge(pht_ready, o.t + 1)
                after(act, gram_ready, o.t)
                a(pht[:, :], p_m0[0:CD, 0:P], ACT.Copy).then_inc(pht_kept, 1)

            def exp_logits(o):
                act.wait_ge(lg_max, o.t + 1)
                after(act, att_ready, o.t)
                after(act, arec_ready, o.t)
                a(at[:, :], lg[:, 1, :], ACT.Exp, bias=nmx[:, :], scale=-1.0, accum_out=asum[:, 0:1]).then_inc(at_ready, 1)

            def keep_weights(o):
                act.wait_ge(att_ready, o.t + 1)
                after(act, mixed_ready, o.t)
                a(att[:, :], p_m0[:, 0:P], ACT.Copy).then_inc(att_kept, 1)

            def gelu(o, j):
                act.wait_ge(fc_ready, 2 * o.t + j + 1)
                if j == 0:
                    after(act, gn_ready, o.t)
                    act.wait_ge(rs2_ready, o.t + 1)
                a(gl[:, 512 * j:512 * j + 512], p_f[:, j, :], ACT.Gelu, scale=rs2[o.par][:, 1:2]).then_inc(gl_ready, 1)

            def high_z2(o):
                act.wait_ge(z2t_ready, o.t + 1)
                after(act, fc_ready, 2 * o.t)
                a(z2h[:, :, :], p_m0[:, 0:E].rearrange("p (k n) -> p k n", k=KT), ACT.Copy).then_inc(z2h_ready, 1)

            def high_hidden(o, j):
                act.wait_ge(gt_ready, 2 * o.t + j + 1)
                after(act, ff_ready, o.t)
                a(gh[:, 4 * j:4 * j + 4, :], p_f[:, j, :].rearrange("p (m n) -> p m n", n=P), ACT.Copy).then_inc(gh_ready, 1)

            def step(do, once):
                do(high_hidden, 3, 0)
                do(keep_weights, 2)
                do(keep_z1, 1)
                do(high_hidden, 3, 1)
                do(keep_k, 0)
                do(keep_q, 0)
                once(temperature, 0)
                once(magnitudes, 1, 1)
                do(keep_unit, 1)
                do(high_z2, 2)
                do(exp_scores, 0)
                do(charge, 1)
                do(sines, 1)
                do(gelu, 2, 0)
                once(magnitudes, 0, 0)
                do(keep_powers, 1)
                do(gelu, 2, 1)
                do(keep_phi, 1)
                do(keep_context, 0)
                do(exp_logits, 1)

            act.wait_ge(in_qkv, 32)
            steps(act, step)

        @block.tensor
        def _(pe):
            mm = nc.tensor.matmul

            def stacked(o, which, bank_, base, l, start, stop):
                for k in range(KT):
                    for q in range(HQ):
                        last = mm(bank_[32 * q:32 * q + 32, base:base + C], wq[:, which, k, l, :], xt[o.par][:, l, k, q, :],
                                  start=(start and k == 0), stop=(stop and k == KT - 1))
                return last

            def project_qv(o, l):
                pe.wait_ge(x_in[o.par][l], 16 * (o.pair + 1))
                if l == 0:
                    after(pe, q_kept, o.t)
                last = stacked(o, 0, p_qv, C * l, l, True, True)
                if l == HL - 1:
                    last.then_inc(qv_ready, 1)

            def project_k(o, l):
                pe.wait_ge(x_in[o.par][l], 16 * (o.pair + 1))
                if l == 0:
                    after(pe, k_kept, o.t)
                last = stacked(o, 1, p_k, 0, l, l == 0, l == HL - 1)
                if l == HL - 1:
                    last.then_inc(k_ready, 1)

            def blocks(bank_, stationary, moving, part, signal):
                for g in range(G // PARTS * part, G // PARTS * (part + 1)):
                    for q in range(0, P, QP):
                        last = mm(bank_[q:q + QP, N * g:N * g + N],
                                  stationary[q:q + QP, g, :, :].rearrange("p a d -> p (a d)"),
                                  moving[q:q + QP, g, :], start=True, stop=True)
                if part == PARTS - 1:
                    last.then_inc(signal, 1)

            def scores(o, part):
                if part == 0:
                    pe.wait_ge(q_kept, o.t + 1)
                    pe.wait_ge(k_kept, o.t + 1)
                    after(pe, pj_kept, o.t)
                    settle(pe)
                blocks(p_a0, qm, ks, part, s_ready)

            def context(o, part):
                if part == 0:
                    pe.wait_ge(p_turned, o.t + 1)
                    pe.wait_ge(v_masked, o.t + 1)
                    after(pe, an_steps, 6 * o.t)
                    settle(pe)
                blocks(p_a1, vm, pt, part, c_ready)

            def join_heads(o):
                if first(o):
                    pe.wait_ge(in_pack, 16)
                pe.wait_ge(c_kept, o.t + 1)
                pe.wait_ge(s_less, o.t + 1)
                for l in range(HL):
                    last = mm(p_a0[:, 0:E], cx[:, l, :, :].rearrange("p b i -> p (b i)"), wo[:, l, :],
                              start=(l == 0), stop=(l == HL - 1))
                last.then_inc(h0_ready, 1)

            def turn_z1(o):
                pe.wait_ge(z1_ready, o.t + 1)
                pe.wait_ge(c_kept, o.t + 1)
                for k in range(KT):
                    last = nc.tensor.transpose(p_a1[:, P * k:P * k + P], z1[:, P * k:P * k + P], idn)
                last.then_inc(z1t_ready, 1)

            def project_z1(o):
                if first(o):
                    pe.wait_ge(w2_ready, 1)
                pe.wait_ge(z1t_kept, o.t + 1)
                pe.wait_ge(h0_kept, o.t + 1)
                for k in range(KT):
                    last = mm(p_a0[:, 0:PW], z1t[:, k, :], w2[:, k, :], start=(k == 0), stop=(k == KT - 1))
                last.then_inc(pj_ready, 1)

            def turn_unit(o):
                pe.wait_ge(un_ready, o.t + 1)
                pe.wait_ge(z1t_kept, o.t + 1)
                settle(pe)
                nc.tensor.transpose(p_a1[0:SH, 0:P], un[:, :], idn).then_inc(unt_ready, 1)

            def angles(o):
                if first(o):
                    pe.wait_ge(in_feat, 32)
                pe.wait_ge(unt_kept, o.t + 1)
                settle(pe)
                mm(p_a1[0:RF, P:2 * P], om[:, :], unt[:, :], start=True, stop=True).then_inc(an_ready, 1)

            def powers(o):
                if first(o):
                    pe.wait_ge(wc_ready, 1)
                pe.wait_ge(ft_ready, o.t + 1)
                after(pe, h1_ready, o.t)
                mm(p_m1[:, 0:(ORDER + 1) * CD], ft[:, :], wc[:, :, :].rearrange("p m c -> p (m c)"),
                   start=True, stop=True).then_inc(y_ready, 1)

            def turn_phi(o):
                pe.wait_ge(phi_steps, ORDER * (o.t + 1))
                after(pe, z2l_ready, o.t)
                settle(pe)
                nc.tensor.transpose(p_m0[0:CD, 0:P], ho[:, ORDER - 1, :], idn).then_inc(pht_ready, 1)

            def gram(o):
                pe.wait_ge(pht_kept, o.t + 1)
                pe.wait_ge(y_kept, o.t + 1)
                mm(p_m1[:, 0:P], pht[:, :], pht[:, :], start=True, stop=True).then_inc(gram_ready, 1)

            def turn_weights(o):
                pe.wait_ge(at_ready, o.t + 1)
                pe.wait_ge(pht_kept, o.t + 1)
                nc.tensor.transpose(p_m0[:, 0:P], at[:, :], idn).then_inc(att_ready, 1)

            def mix(o):
                pe.wait_ge(att_kept, o.t + 1)
                pe.wait_ge(lg_ready, o.t + 1)
                mm(p_m1[:, 0:E], att[:, :], pj[o.par][:, 0:E], start=True, stop=True).then_inc(mixed_ready, 1)

            def turn_z2(o):
                pe.wait_ge(z2_ready, o.t + 1)
                pe.wait_ge(att_kept, o.t + 1)
                for k in range(KT):
                    last = nc.tensor.transpose(p_m0[:, P * k:P * k + P], z2[:, P * k:P * k + P], idn)
                last.then_inc(z2t_ready, 1)

            def widen(o, j):
                if j == 0:
                    if first(o):
                        pe.wait_ge(cut_ready[0], 1)
                    pe.wait_ge(z2l_ready, o.t + 1)
                    after(pe, res_ready, o.t)
                else:
                    if first(o):
                        pe.wait_ge(b3_ready, 1)
                    after(pe, glo_ready, 2 * o.t)
                for k in range(KT):
                    for n, half in enumerate((z2h, z2l)):
                        last = mm(p_f[:, j, :], half[:, k, :], fc[:, k, 512 * j:512 * j + 512],
                                  start=(k == 0 and n == 0), stop=(k == KT - 1 and n == 1))
                last.then_inc(fc_ready, 1)

            def turn_hidden(o, j):
                if j == 0:
                    pe.wait_ge(gn_ready, o.t + 1)
                for m in range(4 * j, 4 * j + 4):
                    last = nc.tensor.transpose(p_f[:, j, P * (m % 4):P * (m % 4) + P], gn[:, P * m:P * m + P], idn)
                last.then_inc(gt_ready, 1)

            def narrow(o, j):
                if first(o) and j == 0:
                    pe.wait_ge(cut_ready[1], 1)
                pe.wait_ge(glo_ready, 2 * o.t + j + 1)
                for m in range(4 * j, 4 * j + 4):
                    for n, half in enumerate((gh, glo)):
                        last = mm(p_f[:, 0, 0:E], half[:, m, :], pr[:, m, :],
                                  start=(m == 0 and n == 0), stop=(m == HC - 1 and n == 1))
                if j == 1:
                    last.then_inc(ff_ready, 1)

            def merge_weights():
                pe.wait_ge(in_pack, 16)
                pe.wait_ge(bvw_ready, 1)
                for n in range(KT):
                    for k in range(KT):
                        mm(p_m0[:, E * n:E * n + E], mv[:, k, P * n:P * n + P], mo[:, k, :], start=(k == 0), stop=(k == KT - 1))
                for k in range(KT):
                    last = mm(p_m1[:, 0:E], bvw[:, k, :], mo[:, k, :], start=(k == 0), stop=(k == KT - 1))
                last.then_inc(w2_made, 1)

            def total_magnitude(n):
                pe.wait_ge(abs_summed[n], 1)
                pe.wait_ge(ones_set, 1)
                mm(p_f[:, n, 0:1], ones[:, :], absum[:, n:n + 1], start=True, stop=True).then_inc(abs_total[n], 1)

            def narrow_bias():
                pe.wait_ge(lnbw_ready, 1)
                pe.wait_ge(cut_ready[1], 1)
                for m in range(HC):
                    last = mm(p_f[:, 1, 0:E], lnbw[:, m, :], pr[:, m, :].bitcast(F32), start=(m == 0), stop=(m == HC - 1))
                last.then_inc(b3_made, 1)

            def step(do, once):
                do(turn_unit, 2)
                do(turn_z2, 3)
                once(total_magnitude, 2, 1)
                do(scores, 1, 2)
                do(scores, 1, 3)
                do(angles, 2)
                do(widen, 3, 0)
                do(project_k, 0, 0)
                do(project_qv, 0, 0)
                do(widen, 3, 1)
                do(powers, 2)
                do(project_qv, 0, 1)
                do(context, 1, 0)
                do(context, 1, 1)
                do(context, 1, 2)
                do(context, 1, 3)
                do(turn_phi, 2)
                do(gram, 2)
                do(join_heads, 1)
                do(turn_hidden, 3, 0)
                do(project_k, 0, 1)
                do(turn_weights, 2)
                do(turn_z1, 1)
                do(turn_hidden, 3, 1)
                do(mix, 2)
                do(project_z1, 1)
                once(narrow_bias, 2)
                once(merge_weights, 0)
                do(narrow, 3, 0)
                once(total_magnitude, 1, 0)
                do(scores, 0, 0)
                do(narrow, 3, 1)
                do(scores, 0, 1)

            pe.wait_ge(in_qkv, 32)
            steps(pe, step)

        @block.vector
        def _(dve):
            v = nc.vector
            dve.wait_ge(in_qkv, 32)
            v.tensor_scalar(bqm[:, :], col[:, COL_MASK:COL_MASK + HH], col[:, COL_BQ:COL_BQ + 1], None,
                            ALU.mult).then_inc(bqm_ready, 1)

            def constants():
                dve.wait_ge(in_pack, 16)
                v.tensor_scalar(tmp[:, 4:5], part("temp"), 0.0, 0.1, ALU.max, ALU.add).then_inc(temp_dve, 1)
                dve.wait_ge(temp_dve, 1)
                dve.wait_ge(temp_act, 3)
                v.tensor_tensor(tmp[:, 5:6], tmp[:, 4:5], tmp[:, 3:4], ALU.add).then_inc(temp_dve, 1)
                dve.wait_ge(temp_dve, 2)
                v.reciprocal(tmp[:, 6:7], tmp[:, 5:6]).then_inc(temp_dve, 1)
                dve.wait_ge(temp_dve, 3)
                v.tensor_scalar(dec[:, :], part("decay"), tmp[:, 6:7], None, ALU.mult).then_inc(dec_ready, 1)

            def merged_bias():
                dve.wait_ge(in_pack, 16)
                v.tensor_copy(w2[:, :, E:PW], part("m_shell").rearrange("p (k c) -> p k c", k=KT))
                v.tensor_copy(b2[:, E:PW], part("b_shell"))
                dve.wait_ge(w2_made, 1)
                v.tensor_copy(w2[:, :, 0:E], p_m0[:, :].rearrange("p (n e) -> p n e", n=KT))
                v.tensor_tensor(b2[:, 0:E], p_m1[:, 0:E], part("b_out"), ALU.add).then_inc(w2_ready, 1)

            def scaled_features():
                dve.wait_ge(in_feat, 32)
                for m in range(ORDER + 1):
                    last = v.tensor_scalar(wc[:, m, :], wc_raw[:, m, :], MAGS[m] * RFF_SCALE, None, ALU.mult)
                last.then_inc(wc_ready, 1)

            def keep_bias3():
                dve.wait_ge(b3_made, 1)
                v.tensor_copy(b3[:, :], p_f[:, 1, 0:E]).then_inc(b3_ready, 1)

            def ternary(n):
                dve.wait_ge(abs_total[n], 1)
                v.tensor_scalar(thr[:, n:n + 1], p_f[:, n, 0:1], 0.5 / (E * HID), 0.5e-6, ALU.mult,
                                ALU.add).then_inc(thr_steps[n], 1)
                dve.wait_ge(thr_steps[n], 1)
                v.tensor_scalar(thr[:, 2 + n:3 + n], thr[:, n:n + 1], -1.0, None, ALU.mult).then_inc(thr_steps[n], 1)
                dve.wait_ge(thr_steps[n], 2)
                flat = raws[n][:, :, :].rearrange("p a b -> p (a b)")
                if n:
                    dve.wait_ge(cut_ready[0], 1)
                v.tensor_scalar(below[:, :], flat, thr[:, 2 + n:3 + n], None, ALU.is_lt).then_inc(below_ready[n], 1)

            def cut(n):
                dve.wait_ge(below_ready[n], 1)
                flat = raws[n][:, :, :].rearrange("p a b -> p (a b)")
                v.scalar_tensor_tensor(cuts[n][:, :, :].rearrange("p a b -> p (a b)"), flat, thr[:, n:n + 1], below[:, :],
                                       ALU.is_gt, ALU.subtract).then_inc(cut_ready[n], 1)

            def turn_v(o):
                dve.wait_ge(qv_ready, o.t + 1)
                v.transpose(qt[:, :, :, :].rearrange("p b l e -> p l b e"),
                            p_qv[:, :].rearrange("p (l b e) -> p l b e", l=HL, b=TB)).then_inc(v_turned, 1)
                dve.wait_ge(v_turned, o.t + 1)
                after(dve, c_ready, o.t)
                vs = qt[:, :, :, :].rearrange("p b l e -> p b (l e)")[:, :, D:3 * D].rearrange("p b (l d) -> p b l d", l=HL)
                for h in range(HH):
                    last = v.tensor_scalar(vm[:, :, h, :].rearrange("p (b l) d -> p b l d", l=HL), vs,
                                           col[:, COL_MASK + h:COL_MASK + h + 1], None, ALU.mult)
                last.then_inc(v_masked, 1)

            def less_max(o):
                dve.wait_ge(s_ready, o.t + 1)
                grouped = p_a0[:, 0:C].rearrange("p (g n) -> p g n", g=G)
                v.tensor_reduce(smax[:, :], grouped, AX.X, ALU.max).then_inc(s_max, 1)
                dve.wait_ge(s_max, o.t + 1)
                after(dve, s_exp, o.t)
                v.tensor_tensor(sc[:, :, :], grouped, smax[:, :].unsqueeze(2).to_broadcast([P, G, N]),
                                ALU.subtract).then_inc(s_less, 1)

            def probabilities(o):
                dve.wait_ge(s_exp, o.t + 1)
                v.tensor_reduce(ssum[:, :], pe_[:, :, :], AX.X, ALU.add).then_inc(s_sum, 1)
                dve.wait_ge(s_sum, o.t + 1)
                v.reciprocal(srec[:, :], ssum[:, :]).then_inc(s_rec, 1)
                dve.wait_ge(s_rec, o.t + 1)
                v.tensor_tensor(pn[:, :, :], pe_[:, :, :], srec[:, :].unsqueeze(2).to_broadcast([P, G, N]),
                                ALU.mult).then_inc(p_ready, 1)
                dve.wait_ge(p_ready, o.t + 1)
                after(dve, c_ready, o.t)
                v.transpose(pt[:, :, :].rearrange("p g n -> p (g n)"),
                            pn[:, :, :].rearrange("p g n -> p (g n)")).then_inc(p_turned, 1)

            def keep_h0(o):
                dve.wait_ge(h0_ready, o.t + 1)
                after(dve, h1_ready, o.t - 1)
                v.tensor_tensor(h0[o.par][:, :], p_a0[:, 0:E], bo, ALU.add).then_inc(h0_kept, 1)
                dve.wait_ge(h0_kept, o.t + 1)
                v.bn_stats(st1[:, :], h0[o.par][:, :]).then_inc(st1_ready, 1)
                dve.wait_ge(st1_ready, o.t + 1)
                after(dve, var1_ready, o.t)
                settle(dve)
                v.bn_aggr(mv1[:, :], st1[:, :]).then_inc(mv1_ready, 1)

            def center1(o):
                dve.wait_ge(mv1_ready, o.t + 1)
                after(dve, z1t_ready, o.t)
                v.tensor_scalar(z1[:, :], h0[o.par][:, :], mv1[:, 0:1], None, ALU.subtract).then_inc(z1_ready, 1)

            def keep_projection(o):
                if first(o):
                    dve.wait_ge(w2_ready, 1)
                dve.wait_ge(pj_ready, o.t + 1)
                after(dve, mixed_ready, o.t - 1)
                after(dve, charge_ready, o.t - 1)
                dve.wait_ge(rs1_ready, o.t + 1)
                v.scalar_tensor_tensor(pj[o.par][:, :], p_a0[:, 0:PW], rs1[:, 1:2], b2[:, :], ALU.mult,
                                       ALU.add).then_inc(pj_kept, 1)
                dve.wait_ge(pj_kept, o.t + 1)
                after(dve, floor_ready, o.t)
                shell = pj[o.par][:, E:E + SH]
                v.tensor_tensor_reduce(sq[:, :], shell, shell, 1.0, 0.0, ALU.mult, ALU.add, nn[:, 0:1]).then_inc(n2_ready, 1)

            def unit(o):
                dve.wait_ge(rn_ready, o.t + 1)
                after(dve, unt_ready, o.t)
                v.tensor_scalar(un[:, :], pj[o.par][:, E:E + SH], nn[:, 2:3], None, ALU.mult).then_inc(un_ready, 1)

            def reduce_angles(o):
                dve.wait_ge(an_ready, o.t + 1)
                n = 6 * o.t
                v.tensor_scalar(ang[:, 0, :], p_a1[0:RF, P:2 * P], col[0:RF, COL_RB:COL_RB + 1], None,
                                ALU.add).then_inc(an_steps, 1)
                dve.wait_ge(an_steps, n + 1)
                v.tensor_scalar(ang[:, 1, :], ang[:, 0, :], 0.5 / math.pi, col[0:RF, COL_OFF:COL_OFF + 1], ALU.mult,
                                ALU.add).then_inc(an_steps, 1)
                dve.wait_ge(an_steps, n + 2)
                v.tensor_scalar(ang[:, 2, :], ang[:, 1, :], MAGIC, MAGIC, ALU.add, ALU.subtract).then_inc(an_steps, 1)
                dve.wait_ge(an_steps, n + 3)
                v.scalar_tensor_tensor(ang[:, 3, :], ang[:, 2, :], -TWO_PI_HI, ang[:, 0, :], ALU.mult,
                                       ALU.add).then_inc(an_steps, 1)
                dve.wait_ge(an_steps, n + 4)
                v.scalar_tensor_tensor(ang[:, 1, :], ang[:, 2, :], -TWO_PI_LO, ang[:, 3, :], ALU.mult,
                                       ALU.add).then_inc(an_steps, 1)
                dve.wait_ge(an_steps, n + 5)
                after(dve, ft_ready, o.t)
                v.tensor_scalar(ang[:, 4, :], ang[:, 1, :], col[0:RF, COL_HI:COL_HI + 1], col[0:RF, COL_LO:COL_LO + 1],
                                ALU.min, ALU.max).then_inc(an_steps, 1)

            def combine(o):
                dve.wait_ge(y_kept, o.t + 1)
                dve.wait_ge(charge_ready, o.t + 1)
                after(dve, pht_ready, o.t)
                for m in range(ORDER):
                    src = yy[:, ORDER, :] if m == 0 else ho[:, m - 1, :]
                    if m:
                        dve.wait_ge(phi_steps, ORDER * o.t + m)
                    v.scalar_tensor_tensor(ho[:, m, :], src, qc[o.par][:, :], yy[:, ORDER - 1 - m, :], ALU.mult,
                                           ALU.add).then_inc(phi_steps, 1)

            def logits(o):
                if first(o):
                    dve.wait_ge(dec_ready, 1)
                dve.wait_ge(gram_ready, o.t + 1)
                after(dve, at_ready, o.t)
                v.tensor_tensor(lg[:, 0, :], p_m1[:, 0:P], dec[:, :], ALU.mult).then_inc(lg_ready, 1)
                dve.wait_ge(lg_ready, o.t + 1)
                settle(dve)
                v.tensor_tensor_reduce(lg[:, 1, :], lg[:, 0, :], hid, -1.0, 3e38, ALU.add, ALU.min,
                                       nmx[:, :]).then_inc(lg_max, 1)

            def residual(o):
                dve.wait_ge(at_ready, o.t + 1)
                v.reciprocal(asum[:, 1:2], asum[:, 0:1]).then_inc(arec_ready, 1)
                dve.wait_ge(mixed_ready, o.t + 1)
                dve.wait_ge(arec_ready, o.t + 1)
                after(dve, res_ready, o.t - 1)
                v.scalar_tensor_tensor(h1[o.par][:, :], p_m1[:, 0:E], asum[:, 1:2], h0[o.par][:, :], ALU.mult,
                                       ALU.add).then_inc(h1_ready, 1)
                dve.wait_ge(h1_ready, o.t + 1)
                v.bn_stats(st2[:, :], h1[o.par][:, :]).then_inc(st2_ready, 1)
                dve.wait_ge(st2_ready, o.t + 1)
                after(dve, var2_ready, o.t)
                settle(dve)
                v.bn_aggr(mv2[:, :], st2[:, :]).then_inc(mv2_ready, 1)

            def center2(o):
                dve.wait_ge(mv2_ready, o.t + 1)
                after(dve, z2t_ready, o.t)
                v.tensor_scalar(z2[:, :], h1[o.par][:, :], mv2[:, 0:1], None, ALU.subtract).then_inc(z2_ready, 1)

            def low_z2(o):
                dve.wait_ge(z2h_ready, o.t + 1)
                after(dve, fc_ready, 2 * o.t)
                v.tensor_tensor(z2l[:, :, :], p_m0[:, 0:E].rearrange("p (k n) -> p k n", k=KT), z2h[:, :, :].bitcast(F32),
                                ALU.subtract).then_inc(z2l_ready, 1)

            def stats3(o, j):
                dve.wait_ge(gl_ready, 2 * o.t + j + 1)
                v.bn_stats(st3[:, 6 * j:6 * j + 6], gl[:, 512 * j:512 * j + 512]).then_inc(st3_ready, 1)
                if j:
                    dve.wait_ge(st3_ready, 2 * o.t + 2)
                    after(dve, var3_ready, o.t)
                    settle(dve)
                    v.bn_aggr(mv3[:, :], st3[:, :]).then_inc(mv3_ready, 1)

            def center3(o):
                dve.wait_ge(mv3_ready, o.t + 1)
                if first(o):
                    dve.wait_ge(in_lnw, 16)
                after(dve, gt_ready, 2 * o.t)
                v.scalar_tensor_tensor(gn[:, :], gl[:, :], mv3[:, 0:1], lnw[:, :], ALU.subtract, ALU.mult).then_inc(gn_ready, 1)

            def low_hidden(o, j):
                dve.wait_ge(gh_ready, 2 * o.t + j + 1)
                after(dve, ff_ready, o.t)
                v.tensor_tensor(glo[:, 4 * j:4 * j + 4, :], p_f[:, j, :].rearrange("p (m n) -> p m n", n=P),
                                gh[:, 4 * j:4 * j + 4, :].bitcast(F32), ALU.subtract).then_inc(glo_ready, 1)

            def result(o):
                dve.wait_ge(ff_ready, o.t + 1)
                dve.wait_ge(rs3_ready, o.t + 1)
                dve.wait_ge(h1_biased, o.t + 1)
                after(dve, stored, 16 * o.t)
                v.scalar_tensor_tensor(res[:, :], p_f[:, 0, 0:E], rs3[:, 1:2], h1[o.par][:, :], ALU.mult,
                                       ALU.add).then_inc(res_ready, 1)

            def step(do, once):
                once(keep_bias3, 3)
                do(low_z2, 3)
                once(ternary, 2, 0)
                do(less_max, 1)
                do(reduce_angles, 2)
                once(scaled_features, 2)
                do(probabilities, 1)
                do(stats3, 3, 0)
                do(combine, 2)
                do(stats3, 3, 1)
                once(cut, 2, 0)
                do(center3, 3)
                once(ternary, 2, 1)
                do(logits, 2)
                do(keep_h0, 1)
                do(center1, 1)
                once(constants, 1)
                do(low_hidden, 3, 0)
                do(turn_v, 0)
                once(cut, 2, 1)
                do(low_hidden, 3, 1)
                do(keep_projection, 1)
                do(residual, 2)
                do(unit, 1)
                once(merged_bias, 0)
                do(center2, 2)
                do(result, 3)

            steps(dve, step)


def kernel(**inputs):
    import numpy as np
    import concourse.bacc as bacc
    from concourse.bass_utils import run_bass_kernel_spmd as run

    def take(name):
        return np.asarray(inputs[name])

    nc = bacc.Bacc("TRN2", target_bir_lowering=False, num_devices=1)
    f4 = np.float32
    x = take("x").reshape(TILES, TB, N, HQ, HM, HL, KT, P).transpose(0, 7, 5, 6, 3, 1, 4, 2).reshape(TILES, P, HL, KT, HQ, C)

    def by_k(w):
        return w.T.reshape(w.shape[1] // P, P, w.shape[0]).transpose(1, 0, 2)

    wq, wk, wv = [by_k(take(f"L0_tok_W{n}")) for n in "qkv"]
    none = np.zeros_like(wk)
    pairs = [[(wq, wv), (wv, wq)], [(wk, none), (none, wk)]]
    qkv = np.stack([np.stack([np.concatenate(p, axis=2) for p in row], axis=2) for row in pairs], axis=1)
    wo = take("L0_tok_Wo").T.reshape(HQ, HM, HL, D, E).transpose(0, 1, 3, 2, 4).reshape(P, HL, E)
    rows = lambda v: np.broadcast_to(v.reshape(1, -1), (P, v.size))

    cols = np.zeros((P, COLS), f4)
    cols[:, COL_MASK:COL_MASK + HH] = (np.arange(P)[:, None] // D) % HH == np.arange(HH)
    for c, n in ((COL_BQ, "q"), (COL_BK, "k"), (COL_BV, "v")):
        cols[:, c] = np.tile(take(f"L0_tok_b{n}"), P // D)
    cols[:RF, COL_RB] = np.tile(take("L0_attn_rff_bias"), 2)
    cosine = np.arange(RF) < RF // 2
    cols[:RF, COL_OFF] = np.where(cosine, 0.25, 0.0)
    cols[:RF, COL_SHIFT] = np.where(cosine, HALF_PI, 0.0)
    cols[:RF, COL_HI] = np.where(cosine, PI_IN - HALF_PI, PI_IN)
    cols[:RF, COL_LO] = np.where(cosine, -PI_IN - HALF_PI, -PI_IN)
    cols[:, COL_MBV:COL_MBV + KT] = take("L0_attn_b_v").reshape(KT, P).T
    cols[:, COL_LNB:COL_LNB + HC] = take("L0_ffn_ln_b").reshape(HC, P).T

    tok = np.arange(P)
    seen = (tok[:, None] // N == tok[None, :] // N) & (tok[:, None] >= tok[None, :])
    decay = np.where(seen, np.exp(-0.3 * np.abs(tok[:, None] - tok[None, :]) / 10.0), 0.0).astype(f4)
    hidden = np.where(seen, 0.0, -1e30).astype(f4)

    w_v = take("L0_attn_W_v").reshape(KT, P, E).transpose(1, 0, 2)
    comb = take("L0_attn_W_combine").reshape(CD, ORDER + 1, RF).transpose(2, 1, 0)
    omega = np.tile(take("L0_attn_omega").T, (1, 2))
    parts = {
        "ident": np.eye(P, dtype=f4), "w_o": wo, "b_o": rows(take("L0_tok_bo")), "m_out": by_k(take("L0_attn_W_out")),
        "m_v": w_v, "m_shell": by_k(np.concatenate([take("L0_attn_W_shell"), take("L0_attn_W_charge")])),
        "b_out": rows(take("L0_attn_b_out")),
        "b_shell": rows(np.concatenate([take("L0_attn_b_shell"), take("L0_attn_b_charge")])),
        "temp": rows(take("L0_attn_log_temp")), "decay": decay, "hidden": hidden,
    }
    packed = np.concatenate([parts[n].reshape(P, -1) for n in PACK], axis=1)
    arrays = {
        "x": x, "cols": cols, "w_qkv": qkv, "packed": packed, "omega": omega, "w_comb": comb,
        "w_fc": by_k(take("L0_ffn_W_fc")), "w_proj": by_k(take("L0_ffn_W_proj")), "ln_w": rows(take("L0_ffn_ln_w")),
    }
    arrays = {f"in_{n}": np.ascontiguousarray(a) for n, a in arrays.items()}
    args = [nc.dram_tensor(n, a.shape, mybir.dt.from_np(a.dtype), kind="ExternalInput").ap() for n, a in arrays.items()]
    out = nc.dram_tensor("out_0", (TILES, P, E), F32, kind="ExternalOutput").ap()
    audio_tower(nc, *args, out)
    r = run(nc, [arrays], core_ids=[0])
    return r.results[0]["out_0"].reshape(B, N, E)
```
